# Optimizing a Trainium2 kernel written in Bass

```python
import numpy as np
import jax
import jax.numpy as jnp

def _softmax(x, axis=-1):
    return jax.nn.softmax(x, axis=axis)

def _gelu(x):
    return jax.nn.gelu(x, approximate=True)

def _silu(x):
    return jax.nn.silu(x)

def _sigmoid(x):
    return jax.nn.sigmoid(x)

def _layernorm(x, axis=-1, eps=1e-05):
    m = jnp.mean(x, axis=axis, keepdims=True)
    v = jnp.var(x, axis=axis, keepdims=True)
    return (x - m) / jnp.sqrt(v + eps)

def _scatter_add(tgt, idx, src, axis=0):
    return tgt.at[idx].add(src)

def _segment_sum(src, seg, n):
    return jax.ops.segment_sum(src, seg, n)
kernel_name = 'mk_adj_preln_d1_adj_r2_d63544'

def setup_inputs(seed: int=0):
    np.random.seed(seed)
    _w = jnp.asarray

    def _rec_inputs():
        import jax
        import jax.numpy as jnp
        _gk = jax.random.key(seed)
        x = -0.0001538 + 1 * jax.random.normal(jax.random.fold_in(_gk, 1), (128, 128, 384), jnp.float32)
        _a = jax.random.bernoulli(jax.random.fold_in(_gk, 2), 0.03125, (128, 128, 128))
        _a = jnp.logical_or(_a, jnp.swapaxes(_a, -1, -2))
        _a = jnp.logical_or(_a, jnp.eye(128, dtype=bool))
        adj = _a
        return (x, adj)
    x, adj = _rec_inputs()

    def _L0_gnn_setup():
        import jax, jax.numpy as jnp
        import numpy as np
        B, S, H = (4, 1024, 384)
        NUM_HEADS = 6
        HEAD_SIZE = H // NUM_HEADS
        NEG = -9000000000000000.0

        def _heads(x):
            b, s, _ = x.shape
            return x.reshape(b, s, NUM_HEADS, HEAD_SIZE).transpose(0, 2, 1, 3)
        key = jax.random.key(seed)
        ks = jax.random.split(key, 10)
        seq_inputs = jax.random.normal(ks[0], (B, S, H), dtype=jnp.float32)
        gm = jax.random.randint(ks[1], (B, S, S), 0, 2) > 0
        graph_mask = gm | jnp.eye(S, dtype=bool)[None]
        sc = 1.0 / np.sqrt(H)
        Wq = jax.random.normal(ks[2], (H, H), dtype=jnp.float32) * sc
        bq = jnp.zeros((H,), dtype=jnp.float32)
        Wk = jax.random.normal(ks[3], (H, H), dtype=jnp.float32) * sc
        bk = jnp.zeros((H,), dtype=jnp.float32)
        Wv = jax.random.normal(ks[4], (H, H), dtype=jnp.float32) * sc
        bv = jnp.zeros((H,), dtype=jnp.float32)
        Wf = jax.random.normal(ks[5], (H, H), dtype=jnp.float32) * sc
        bf = jnp.zeros((H,), dtype=jnp.float32)
        return {'seq_inputs': seq_inputs, 'Wq': Wq, 'bq': bq, 'Wk': Wk, 'bk': bk, 'Wv': Wv, 'bv': bv, 'Wf': Wf, 'bf': bf, 'graph_mask': graph_mask}
    _L0_gnn_all = _L0_gnn_setup()
    _L0_gnn_in = {k: v for k, v in _L0_gnn_all.items() if k in ('Wq', 'bq', 'Wk', 'bk', 'Wv', 'bv', 'Wf', 'bf')}
    del _L0_gnn_all
    return {'x': x, 'adj': adj, 'L0_gnn_Wq': _L0_gnn_in['Wq'], 'L0_gnn_bq': _L0_gnn_in['bq'], 'L0_gnn_Wk': _L0_gnn_in['Wk'], 'L0_gnn_bk': _L0_gnn_in['bk'], 'L0_gnn_Wv': _L0_gnn_in['Wv'], 'L0_gnn_bv': _L0_gnn_in['bv'], 'L0_gnn_Wf': _L0_gnn_in['Wf'], 'L0_gnn_bf': _L0_gnn_in['bf']}

def reference(x, adj, L0_gnn_Wq, L0_gnn_bq, L0_gnn_Wk, L0_gnn_bk, L0_gnn_Wv, L0_gnn_bv, L0_gnn_Wf, L0_gnn_bf):
    import jax
    import jax.numpy as jnp

    def _L0_gnn_ref(seq_inputs, Wq, bq, Wk, bk, Wv, bv, Wf, bf, graph_mask):
        import jax, jax.numpy as jnp
        import numpy as np
        B, S, H = (4, 1024, 384)
        NUM_HEADS = 6
        HEAD_SIZE = H // NUM_HEADS
        NEG = -9000000000000000.0

        def _heads(x):
            b, s, _ = x.shape
            return x.reshape(b, s, NUM_HEADS, HEAD_SIZE).transpose(0, 2, 1, 3)
        q = _heads(seq_inputs @ Wq + bq)
        k = _heads(seq_inputs @ Wk + bk)
        v = _heads(seq_inputs @ Wv + bv)
        scores = jnp.einsum('bhqd,bhkd->bhqk', q, k) / np.sqrt(HEAD_SIZE)
        bias = jnp.where(graph_mask, 0.0, NEG)[:, None]
        probs = jax.nn.softmax(scores + bias, axis=-1)
        ctx = jnp.einsum('bhqk,bhkd->bhqd', probs, v)
        ctx = ctx.transpose(0, 2, 1, 3).reshape(seq_inputs.shape[0], seq_inputs.shape[1], H)
        return ctx @ Wf + bf
    h = jnp.maximum(_layernorm(x, axis=-1), 0.0)
    x = x + _L0_gnn_ref(h, L0_gnn_Wq, L0_gnn_bq, L0_gnn_Wk, L0_gnn_bk, L0_gnn_Wv, L0_gnn_bv, L0_gnn_Wf, L0_gnn_bf, adj)
    return x

_drawn_inputs = setup_inputs


def setup_inputs(seed=0):
    import zlib

    import numpy as np

    out = dict(_drawn_inputs(seed))
    spreads = {'L0_gnn_bq': (0.0, 0.784),
     'L0_gnn_bk': (0.0, 0.8),
     'L0_gnn_bv': (0.0, 0.1),
     'L0_gnn_bf': (0.0, 0.1)}
    factors = {}
    for name, (base, spread) in spreads.items():
        noise = np.random.default_rng([zlib.crc32(name.encode()), seed]).standard_normal(out[name].shape)
        drawn = base * np.exp(spread * noise) if base else spread * noise
        out[name] = jnp.asarray(drawn.astype(out[name].dtype))
    for name, factor in factors.items():
        out[name] = (out[name] * factor).astype(out[name].dtype)
    return out
```

```python
from contextlib import ExitStack

import concourse.bass as bass
from concourse import mybir

ALU = mybir.AluOpType
ACT = mybir.ActivationFunctionType
F32 = mybir.dt.float32
F16 = mybir.dt.float16
BF16 = mybir.dt.bfloat16
U8 = mybir.dt.uint8
U32 = mybir.dt.uint32
AX_X = mybir.AxisListType.X
RMAX = bass.bass_isa.ReduceOp.max

P = 128
HEADS = 6
EPS = 1e-5
NEG = -9000000000000000.0

H_UP = 4.0
W_UP = 8.0
UP = H_UP * W_UP

PROJ_AHEAD = 2
HT_AHEAD = 4
NORM_AHEAD = 6
BIAS_AHEAD = 2
RING = 8
UNROLL = 4


def gnn_kernel(nc: bass.Bass, x, adj, Wq, bq, Wk, bk, Wv, bv, Wf, bf, out):
    B, S, H = x.shape
    D = H // HEADS
    C = H // P
    PAIR = 2 * S
    V1 = D + 1
    assert S == P and C * P == H and B % UNROLL == 0

    x_pair = x.rearrange("(n a) t h -> n t a h", a=2)
    adj_pair = adj.rearrange("(n a) q k -> n q a k", a=2)
    out_pair = out.rearrange("(n a) t h -> n t a h", a=2)

    with ExitStack() as ctx:
        def sb(name, shape, dt):
            return ctx.enter_context(nc.sbuf_tensor(name, shape, dt))

        def psum(name, shape):
            return ctx.enter_context(nc.psum_tensor(name, shape, F32))

        def sem(name):
            return ctx.enter_context(nc.semaphore(name))

        w_raw = sb("w_raw", [P, 4, C, H], F32)
        w_hi = sb("w_hi", [P, 4, C, H], F16)
        w_lo = sb("w_lo", [P, 4, C, H], F16)
        b_raw = sb("b_raw", [P, 3, C], F32)
        b_up = sb("b_up", [P, 2, C], F32)
        bv_wide = sb("bv_wide", [P, C, P], F32)
        bf_rows = sb("bf_rows", [P, H], F32)
        out_bias = sb("out_bias", [P, H], F32)
        ident = sb("ident", [P, P], F32)
        ident_bf = sb("ident_bf", [P, P], BF16)
        peak = sb("peak", [P, 8], F32)
        peak_all = sb("peak_all", [P, 8], F32)
        size = sb("size", [P, 4], F32)
        pow2 = sb("pow2", [P, 4], F32)
        pow2_inv = sb("pow2_inv", [P, 4], F32)
        w_scale = sb("w_scale", [P, 4], F32)
        consts = sb("consts", [P, 8], F32)
        exponent = sb("exponent", [P, 1], F32)
        x_in = sb("x_in", [P, 2, 2, H], F32)
        adj_in = sb("adj_in", [P, 2, 2, S], U8)
        stats = sb("stats", [P, 4, 6], F32)
        mean_var = sb("mean_var", [P, 4, 2], F32)
        neg_mean = sb("neg_mean", [P, 4], F32)
        var_eps = sb("var_eps", [P, 4], F32)
        rstd = sb("rstd", [P, 4], F32)
        shift = sb("shift", [P, 4], F32)
        x_norm = sb("x_norm", [P, 4, H], F32)
        resid = sb("resid", [P, RING * H], F32)
        mask = sb("mask", [P, 4, S], BF16)
        h_hi = sb("h_hi", [P, 2, C, PAIR], F16)
        h_lo = sb("h_lo", [P, 2, C, PAIR], F16)
        qk_hi = sb("qk_hi", [P, 2, 2, C, PAIR], F16)
        qk_lo = sb("qk_lo", [P, 2, 2, C, PAIR], F16)
        v_hi = sb("v_hi", [P, 4, HEADS, V1], F16)
        v_lo = sb("v_lo", [P, 4, HEADS, V1], F16)
        row_max = sb("row_max", [P, 2, C], F32)
        probs = sb("probs", [P, 2, C, S], F32)
        pt_hi = sb("pt_hi", [P, HEADS, S], F16)
        pt_lo = sb("pt_lo", [P, HEADS, S], F16)
        inv_sum = sb("inv_sum", [P, HEADS], F32)
        context = sb("context", [P, H], F32)
        ct_hi = sb("ct_hi", [P, C, S], F16)
        ct_lo = sb("ct_lo", [P, C, S], F16)
        y_out = sb("y_out", [P, 2, 2, H], F32)

        ps_scores = psum("ps_scores", [P, 2, 512])
        ps_pt = psum("ps_pt", [P, 2, 512])
        ps_proj = [psum(f"ps_proj{i}", [P, 512]) for i in range(2)]
        ps_ctx = psum("ps_ctx", [P, 512])
        ps_turn = psum("ps_turn", [P, 512])
        scores = ps_scores[:, :, 0:C * S].rearrange("p r (c k) -> p r c k", c=C)
        pt = ps_pt[:, :, :].rearrange("p b n -> p (b n)")[:, 0:HEADS * S].rearrange(
            "p (h k) -> p h k", h=HEADS)
        ctx_sum = ps_ctx[:, 0:HEADS * V1].rearrange("p (h d) -> p h d", h=HEADS)
        turn = ps_turn[:, 0:H].rearrange("p (c t) -> p c t", c=C)

        s_weights = sem("s_weights")
        s_small = sem("s_small")
        s_x = [sem(f"s_x{i}") for i in range(2)]
        s_adj = [sem(f"s_adj{i}") for i in range(2)]
        s_store = [sem(f"s_store{i}") for i in range(2)]
        s_ident = sem("s_ident")
        s_peak = sem("s_peak")
        s_peak_all = sem("s_peak_all")
        s_scale = sem("s_scale")
        s_w_hi = sem("s_w_hi")
        s_w_lo = sem("s_w_lo")
        s_bv_wide = sem("s_bv_wide")
        s_bvwf = sem("s_bvwf")
        s_out_bias = sem("s_out_bias")
        s_ones = sem("s_ones")
        s_moments = sem("s_moments")
        s_mean_var = sem("s_mean_var")
        s_stats = sem("s_stats")
        s_rstd = sem("s_rstd")
        s_shift = sem("s_shift")
        s_norm = sem("s_norm")
        s_resid = sem("s_resid")
        s_mask = sem("s_mask")
        s_turn_h = sem("s_turn_h")
        s_h_hi = sem("s_h_hi")
        s_h_lo = sem("s_h_lo")
        s_chunk = [sem(f"s_chunk{i}") for i in range(3)]
        s_chunk_hi = [sem(f"s_chunk_hi{i}") for i in range(3)]
        s_chunk_lo = [sem(f"s_chunk_lo{i}") for i in range(3)]
        s_v = sem("s_v")
        s_v_hi = sem("s_v_hi")
        s_v_lo = sem("s_v_lo")
        s_scores = sem("s_scores")
        s_max = sem("s_max")
        s_sub = sem("s_sub")
        s_exp = sem("s_exp")
        s_turn_p = sem("s_turn_p")
        s_pt_hi = sem("s_pt_hi")
        s_pt_lo = sem("s_pt_lo")
        s_pv = sem("s_pv")
        s_inv = sem("s_inv")
        s_context = sem("s_context")
        s_turn_c = sem("s_turn_c")
        s_ct_hi = sem("s_ct_hi")
        s_ct_lo = sem("s_ct_lo")
        s_y = sem("s_y")
        s_out = sem("s_out")

        def done(eng, semaphore, k):
            if not isinstance(k, int) or k >= 0:
                eng.wait_ge(semaphore, k + 1)

        def landed(eng, semaphore, turn_no):
            if not isinstance(turn_no, int) or turn_no >= 0:
                eng.wait_ge(semaphore, turn_no * 16 + 16)

        def has(g):
            return not isinstance(g, int) or 0 <= g < B

        FIRST = -NORM_AHEAD
        LOOP_FROM, LOOP_TO = UNROLL, B - 3 * UNROLL
        LAST = B

        def run_slots(eng, slot):
            for g in range(FIRST, LOOP_FROM):
                slot(g, g % UNROLL)
            with eng.Fori(LOOP_FROM, LOOP_TO - UNROLL + 1, UNROLL) as g0:
                for s in range(UNROLL):
                    slot(g0 + s if s else g0, s)
            for g in range(LOOP_TO, LAST + 1):
                slot(g, g % UNROLL)

        def at(s, ahead):
            return (s + ahead) % 4

        def pair_of(s, ahead):
            return at(s, ahead) // 2, at(s, ahead) % 2

        def proj_bank(s, use):
            return ps_proj[(s + use) % 2]

        def split_matmuls(o, pairs, start, stop):
            for i, (w, m) in enumerate(pairs):
                last = nc.tensor.matmul(o, w, m, start=start and i == 0, stop=stop and i == len(pairs) - 1)
            return last

        block = ctx.enter_context(nc.Block())

        @block.sync
        def _(sp):
            def load_x(n, parity):
                sp.dma_start(x_in[:, parity, :, :], x_pair[n]).then_inc(s_x[parity], 16)

            def load_adj(n, parity):
                sp.dma_start(adj_in[:, parity, :, :], adj_pair[n]).then_inc(s_adj[parity], 16)

            for n in range(2):
                load_x(n, n)
            for i, b in enumerate((bq, bk, bv)):
                sp.dma_start(b_raw[:, i, :], b.rearrange("(c p) -> p c", p=P), allow_slow_non_contiguous=True).then_inc(s_small, 16)
            sp.dma_start(bf_rows[:, :], bf.rearrange("(a n) -> a n", a=1).broadcast_to([P, H])).then_inc(s_small, 16)
            for n in range(2):
                load_adj(n, n)

            def slot(g, s):
                if s % 2:
                    return
                n = g // 2 if isinstance(g, int) else g >> 1
                parity, _ = pair_of(s, NORM_AHEAD)
                if has(g + NORM_AHEAD + 4):
                    done(sp, s_norm, g + NORM_AHEAD + 1)
                    done(sp, s_resid, g + NORM_AHEAD + 1)
                    load_x(n + NORM_AHEAD // 2 + 2, parity)
                parity, _ = pair_of(s, BIAS_AHEAD)
                if has(g + BIAS_AHEAD + 4) and has(g + BIAS_AHEAD):
                    done(sp, s_mask, g + BIAS_AHEAD + 1)
                    load_adj(n + BIAS_AHEAD // 2 + 2, parity)
                if has(g - 2):
                    parity, _ = pair_of(s, -2)
                    done(sp, s_out, g - 1)
                    sp.dma_start(out_pair[n - 1], y_out[:, parity, :, :]).then_inc(s_store[parity], 16)

            run_slots(sp, slot)
            for parity in range(2):
                sp.wait_ge(s_store[parity], 16 * (B // 4))

        @block.gpsimd
        def _(pool):
            nc.gpsimd.memset(ident[:, :], 0.0).then_inc(s_ident, 1)
            nc.gpsimd.memset(ident_bf[:, :], 0.0).then_inc(s_ident, 1)
            nc.gpsimd.memset(exponent[:, :], -0.5).then_inc(s_ident, 1)
            pool.wait_ge(s_ident, 3)
            for m in (ident, ident_bf):
                nc.gpsimd.affine_select(out=m[:, :], in_=m[:, :], compare_op=ALU.not_equal, fill=1.0,
                                        base=0, pattern=[[-1, P]], channel_multiplier=1).then_inc(s_ident, 1)
            nc.gpsimd.memset(v_hi[:, :, :, D:V1], 1.0).then_inc(s_ones, 1)
            pool.wait_ge(s_peak, 4)
            nc.gpsimd.partition_all_reduce(peak_all[:, :], peak[:, :], P, RMAX).then_inc(s_peak_all, 1)

            def slot(g, s):
                m = g + NORM_AHEAD
                if has(m):
                    i = at(s, NORM_AHEAD)
                    parity, a = pair_of(s, NORM_AHEAD)
                    col = slice(i, i + 1)
                    done(pool, s_stats, m)
                    done(pool, s_norm, m - 4)
                    nc.gpsimd.tensor_tensor(rstd[:, col], var_eps[:, col], exponent[:, :], ALU.pow).then_inc(s_rstd, 1)
                    done(pool, s_rstd, m)
                    nc.gpsimd.tensor_tensor(shift[:, col], neg_mean[:, col], rstd[:, col], ALU.mult).then_inc(s_shift, 1)
                    if isinstance(m, int) and m == 0:
                        pool.wait_ge(s_out_bias, 1)
                    done(pool, s_out, m - RING)
                    ring = (m % RING if isinstance(m, int) else m & (RING - 1)) * H
                    nc.gpsimd.tensor_tensor(resid[:, bass.ds(ring, H)], x_in[:, parity, a, :], out_bias[:, :],
                                            ALU.add).then_inc(s_resid, 1)

            run_slots(pool, slot)

        @block.scalar
        def _(act):
            for i, w in enumerate((Wq, Wk, Wv, Wf)):
                act.dma_start(w_raw[:, i, :, :], w.rearrange("(c p) n -> p c n", p=P)).then_inc(s_weights, 16)
            act.wait_ge(s_small, 64)
            nc.scalar.copy(bv_wide[:, :, :], b_raw[:, 2, :].unsqueeze(2).broadcast_to([P, C, P])).then_inc(s_bv_wide, 1)
            act.wait_ge(s_weights, 64)
            act.wait_ge(s_scale, 4)
            for i in range(4):
                nc.scalar.activation(w_hi[:, i, :, :], w_raw[:, i, :, :], ACT.Copy,
                                     scale=w_scale[:, i:i + 1]).then_inc(s_w_hi, 1)
            act.wait_ge(s_scale, 6)

            def slot(g, s):
                k = g + PROJ_AHEAD
                parity, a = pair_of(s, PROJ_AHEAD)

                def norm(m):
                    i = at(s, NORM_AHEAD)
                    xp, xa = pair_of(s, NORM_AHEAD)
                    done(act, s_shift, m)
                    done(act, s_turn_h, m - 4)
                    nc.scalar.activation(x_norm[:, i, :], x_in[:, xp, xa, :], ACT.Identity, bias=shift[:, i:i + 1],
                                         scale=rstd[:, i:i + 1]).then_inc(s_norm, 1)

                def make_mask(m):
                    i = at(s, BIAS_AHEAD)
                    ap, aa = pair_of(s, BIAS_AHEAD)
                    landed(act, s_adj[ap], m // 4 if isinstance(m, int) else m >> 2)
                    done(act, s_scores, m - 4)
                    nc.scalar.activation(mask[:, i, :], adj_in[:, ap, aa, :], ACT.Identity, bias=consts[:, 1:2],
                                         scale=consts[:, 2:3]).then_inc(s_mask, 1)

                def chunk(c):
                    if has(k):
                        done(act, s_chunk[c], k)
                        nc.scalar.activation(qk_hi[:, parity, a, c, :], proj_bank(s, c)[:, 0:PAIR], ACT.Identity,
                                             bias=b_up[:, a, c:c + 1]).then_inc(s_chunk_hi[c], 1)

                chunk(0)
                if has(g):
                    done(act, s_sub, g)
                    nc.scalar.activation(probs[:, :, :, :], probs[:, :, :, :], ACT.Exp,
                                         scale=consts[:, 0:1]).then_inc(s_exp, 1)
                chunk(1)
                if has(g + HT_AHEAD):
                    hp, ha = pair_of(s, HT_AHEAD)
                    done(act, s_turn_h, g + HT_AHEAD)
                    nc.scalar.activation(h_hi[:, hp, :, ha * S:(ha + 1) * S], turn, ACT.Relu).then_inc(s_h_hi, 1)
                chunk(2)
                if has(g + NORM_AHEAD):
                    norm(g + NORM_AHEAD)
                if has(g):
                    done(act, s_turn_p, g)
                    nc.scalar.activation(pt_hi[:, :, :], pt, ACT.Copy).then_inc(s_pt_hi, 1)
                if has(k):
                    done(act, s_v, k)
                    if isinstance(k, int) and k == 0:
                        act.wait_ge(s_ones, 1)
                    nc.scalar.activation(v_hi[:, at(s, PROJ_AHEAD), :, 0:D],
                                         proj_bank(s, 3)[:, 0:H].rearrange("p (h d) -> p h d", h=HEADS),
                                         ACT.Copy).then_inc(s_v_hi, 1)
                if has(g + BIAS_AHEAD):
                    make_mask(g + BIAS_AHEAD)
                if has(g):
                    done(act, s_turn_c, g)
                    nc.scalar.activation(ct_hi[:, :, :], turn, ACT.Copy).then_inc(s_ct_hi, 1)

            run_slots(act, slot)

        @block.vector
        def _(dve):
            dve.wait_ge(s_weights, 64)
            dve.wait_ge(s_small, 64)
            nc.vector.memset(peak[:, 6:8], 0.0).then_inc(s_peak, 1)
            nc.vector.tensor_reduce(peak[:, 0:4], w_raw[:, :, :, :].rearrange("p m c n -> p m (c n)"), AX_X, ALU.max,
                                    apply_absolute_value=True).then_inc(s_peak, 1)
            nc.vector.tensor_reduce(peak[:, 4:6], b_raw[:, 0:2, :], AX_X, ALU.max,
                                    apply_absolute_value=True).then_inc(s_peak, 1)
            dve.wait_ge(s_peak, 3)
            nc.vector.tensor_scalar(peak[:, 4:6], peak[:, 4:6], 1.0 / P, None, ALU.mult).then_inc(s_peak, 1)
            dve.wait_ge(s_peak_all, 1)
            nc.vector.tensor_tensor(peak_all[:, 0:2], peak_all[:, 0:2], peak_all[:, 4:6], ALU.max).then_inc(s_scale, 1)
            dve.wait_ge(s_scale, 1)
            nc.vector.tensor_scalar(size[:, :], peak_all[:, 0:4], 2.0 ** -30, 2.0 ** 40, ALU.max, ALU.min).then_inc(s_scale, 1)
            dve.wait_ge(s_scale, 2)
            nc.vector.tensor_scalar(pow2[:, :].bitcast(U32), size[:, :].bitcast(U32), 0x7F800000, None,
                                    ALU.bitwise_and).then_inc(s_scale, 1)
            dve.wait_ge(s_scale, 3)
            nc.vector.reciprocal(pow2_inv[:, :], pow2[:, :]).then_inc(s_peak, 1)
            dve.wait_ge(s_peak, 5)
            nc.vector.tensor_scalar(w_scale[:, :], pow2_inv[:, :], W_UP, None, ALU.mult).then_inc(s_scale, 1)
            nc.vector.scalar_tensor_tensor(consts[:, 0:1], pow2[:, 0:1], 1.0 / (UP * UP * D ** 0.5), pow2[:, 1:2],
                                           ALU.mult, ALU.mult).then_inc(s_peak, 1)
            for col, value in ((1, NEG), (2, -NEG)):
                nc.vector.scalar_tensor_tensor(consts[:, col:col + 1], pow2_inv[:, 0:1], value * UP * UP * D ** 0.5,
                                               pow2_inv[:, 1:2], ALU.mult, ALU.mult).then_inc(s_peak, 1)
            nc.vector.scalar_tensor_tensor(consts[:, 3:4], pow2[:, 2:3], 1.0 / (UP * W_UP), pow2[:, 3:4],
                                           ALU.mult, ALU.mult).then_inc(s_peak, 1)
            dve.wait_ge(s_peak, 9)
            for i in range(2):
                nc.vector.tensor_scalar(b_up[:, i, :], b_raw[:, i, :], pow2_inv[:, i:i + 1], UP, ALU.mult,
                                        ALU.mult).then_inc(s_scale, 1)
            for i in range(4):
                dve.wait_ge(s_w_hi, i + 1)
                nc.vector.scalar_tensor_tensor(w_lo[:, i, :, :].rearrange("p c n -> p (c n)"),
                                               w_raw[:, i, :, :].rearrange("p c n -> p (c n)"), w_scale[:, i:i + 1],
                                               w_hi[:, i, :, :].rearrange("p c n -> p (c n)"), ALU.mult,
                                               ALU.subtract).then_inc(s_w_lo, 1)
            dve.wait_ge(s_bvwf, 1)
            nc.vector.tensor_tensor(out_bias[:, :], ps_ctx[:, 0:H], bf_rows[:, :], ALU.add).then_inc(s_out_bias, 1)

            def slot(g, s):
                k = g + PROJ_AHEAD
                parity, a = pair_of(s, PROJ_AHEAD)

                def chunk(c):
                    if has(k):
                        done(dve, s_chunk_hi[c], k)
                        nc.vector.scalar_tensor_tensor(qk_lo[:, parity, a, c, :], proj_bank(s, c)[:, 0:PAIR],
                                                       b_up[:, a, c:c + 1], qk_hi[:, parity, a, c, :], ALU.add,
                                                       ALU.subtract).then_inc(s_chunk_lo[c], 1)

                if has(g):
                    done(dve, s_scores, g)
                    nc.vector.tensor_reduce(row_max[:, :, :], scores, AX_X, ALU.max).then_inc(s_max, 1)
                    done(dve, s_max, g)
                    nc.vector.tensor_tensor(probs[:, :, :, :], scores,
                                            row_max[:, :, :].unsqueeze(3).broadcast_to([P, 2, C, S]),
                                            ALU.subtract).then_inc(s_sub, 1)
                m = g + NORM_AHEAD
                if has(m):
                    i = at(s, NORM_AHEAD)
                    xp, xa = pair_of(s, NORM_AHEAD)
                    landed(dve, s_x[xp], m // 4 if isinstance(m, int) else m >> 2)
                    nc.vector.bn_stats(stats[:, i, :], x_in[:, xp, xa, :]).then_inc(s_moments, 1)
                    done(dve, s_moments, m)
                chunk(0)
                if has(m):
                    nc.vector.bn_aggr(mean_var[:, i, :], stats[:, i, :]).then_inc(s_mean_var, 1)
                    done(dve, s_shift, m - 4)
                    done(dve, s_mean_var, m)
                    nc.vector.tensor_scalar(var_eps[:, i:i + 1], mean_var[:, i, 1:2], H_UP ** -2, EPS * H_UP ** -2,
                                            ALU.mult, ALU.add)
                    nc.vector.tensor_scalar(neg_mean[:, i:i + 1], mean_var[:, i, 0:1], -1.0, None,
                                            ALU.mult).then_inc(s_stats, 1)
                chunk(1)
                if has(g + HT_AHEAD):
                    hp, ha = pair_of(s, HT_AHEAD)
                    part = slice(ha * S, (ha + 1) * S)
                    done(dve, s_h_hi, g + HT_AHEAD)
                    nc.vector.scalar_tensor_tensor(h_lo[:, hp, :, part], turn, 0.0, h_hi[:, hp, :, part], ALU.max,
                                                   ALU.subtract).then_inc(s_h_lo, 1)
                chunk(2)
                if has(g):
                    done(dve, s_pt_hi, g)
                    nc.vector.tensor_tensor(pt_lo[:, :, :], pt, pt_hi[:, :, :], ALU.subtract).then_inc(s_pt_lo, 1)
                if has(k):
                    done(dve, s_v_hi, k)
                    i = at(s, PROJ_AHEAD)
                    nc.vector.tensor_tensor(v_lo[:, i, :, 0:D],
                                            proj_bank(s, 3)[:, 0:H].rearrange("p (h d) -> p h d", h=HEADS),
                                            v_hi[:, i, :, 0:D], ALU.subtract).then_inc(s_v_lo, 1)
                if has(g):
                    done(dve, s_pv, g)
                    nc.vector.reciprocal(inv_sum[:, :], ctx_sum[:, :, D]).then_inc(s_inv, 1)
                    done(dve, s_inv, g)
                    nc.vector.tensor_tensor(context[:, :].rearrange("p (h d) -> p h d", h=HEADS), ctx_sum[:, :, 0:D],
                                            inv_sum[:, :].unsqueeze(2).broadcast_to([P, HEADS, D]),
                                            ALU.mult).then_inc(s_context, 1)
                if has(g - 1):
                    i = at(s, -1)
                    op, oa = pair_of(s, -1)
                    done(dve, s_y, g - 1)
                    done(dve, s_resid, g - 1)
                    landed(dve, s_store[op], (g - 1) // 4 - 1 if isinstance(g, int) else ((g - 1) >> 2) - 1)
                    ring = ((g - 1) % RING if isinstance(g, int) else (g - 1) & (RING - 1)) * H
                    nc.vector.scalar_tensor_tensor(y_out[:, op, oa, :], proj_bank(s, 4)[:, 0:H], consts[:, 3:4],
                                                   resid[:, bass.ds(ring, H)], ALU.mult, ALU.add).then_inc(s_out, 1)
                if has(g):
                    done(dve, s_ct_hi, g)
                    nc.vector.tensor_tensor(ct_lo[:, :, :], turn, ct_hi[:, :, :], ALU.subtract).then_inc(s_ct_lo, 1)

            run_slots(dve, slot)

        @block.tensor
        def _(pe):
            pe.wait_ge(s_weights, 64)
            pe.wait_ge(s_bv_wide, 1)
            for c in range(C):
                last = nc.tensor.matmul(ps_ctx[:, 0:H], bv_wide[:, c, :], w_raw[:, 3, c, :], start=(c == 0),
                                        stop=(c == C - 1))
            last.then_inc(s_bvwf, 1)
            pe.wait_ge(s_ident, 5)
            pe.wait_ge(s_w_lo, 4)
            pe.wait_ge(s_out_bias, 1)

            def slot(g, s):
                k = g + PROJ_AHEAD
                parity, a = pair_of(s, PROJ_AHEAD)
                cur, half = pair_of(s, 0)

                def chunk(c):
                    feats = slice(c * P, (c + 1) * P)
                    pairs = []
                    for i in range(C):
                        pairs += [(w_hi[:, a, i, feats], h_hi[:, parity, i, :]),
                                  (w_hi[:, a, i, feats], h_lo[:, parity, i, :]),
                                  (w_lo[:, a, i, feats], h_hi[:, parity, i, :])]
                    split_matmuls(proj_bank(s, c)[:, 0:PAIR], pairs, True, True).then_inc(s_chunk[c], 1)

                if has(g):
                    if half == 0:
                        done(pe, s_chunk_lo[2], g + 1)
                    done(pe, s_mask, g)
                    done(pe, s_sub, g - 1)
                    for r in range(2):
                        nc.tensor.matmul(scores[:, r, :, :], ident_bf[:, :],
                                         mask[:, at(s, 0), :].unsqueeze(1).broadcast_to([P, C, S]),
                                         start=True, stop=False, skip_group_check=True)
                    tok = slice(half * S, (half + 1) * S)
                    for c in range(C):
                        for q, kk in ((qk_hi, qk_hi), (qk_lo, qk_hi), (qk_hi, qk_lo)):
                            for r in range(2):
                                rows = slice(r * D, (r + 1) * D)
                                last = nc.tensor.matmul(scores[:, r, c, :], q[rows, cur, 0, c, tok],
                                                        kk[rows, cur, 1, c, tok], start=False,
                                                        stop=(kk is qk_lo), skip_group_check=True)
                    last.then_inc(s_scores, 1)
                if has(k):
                    if a == 0:
                        done(pe, s_h_lo, k + 1)
                    done(pe, s_v_lo, k - 1)
                    chunk(0)
                    done(pe, s_out, g - 2)
                    chunk(1)
                if has(g + HT_AHEAD):
                    done(pe, s_norm, g + HT_AHEAD)
                    done(pe, s_ct_lo, g - 1)
                    if isinstance(g, int) and g + HT_AHEAD - 1 >= 0:
                        done(pe, s_h_lo, g + HT_AHEAD - 1)
                    for c in range(C):
                        last = nc.tensor.transpose(turn[:, c, :], x_norm[:, at(s, HT_AHEAD), c * P:(c + 1) * P],
                                                   ident[:, :])
                    last.then_inc(s_turn_h, 1)
                if has(k):
                    done(pe, s_chunk_lo[0], k)
                    chunk(2)
                if has(g):
                    done(pe, s_exp, g)
                    done(pe, s_pt_lo, g - 1)
                    for h in range(HEADS):
                        last = nc.tensor.transpose(pt[:, h, :], probs[:, h % 2, h // 2, :], ident[:, :])
                    last.then_inc(s_turn_p, 1)
                if has(k):
                    done(pe, s_chunk_lo[1], k)
                    tok = slice(a * S, (a + 1) * S)
                    pairs = []
                    for i in range(C):
                        pairs += [(h_hi[:, parity, i, tok], w_hi[:, 2, i, :]),
                                  (h_lo[:, parity, i, tok], w_hi[:, 2, i, :]),
                                  (h_hi[:, parity, i, tok], w_lo[:, 2, i, :])]
                    split_matmuls(proj_bank(s, 3)[:, 0:H], pairs, True, True).then_inc(s_v, 1)
                if has(g):
                    done(pe, s_pt_lo, g)
                    done(pe, s_v_lo, g)
                    done(pe, s_context, g - 1)
                    vi = at(s, 0)
                    for h in range(HEADS):
                        nc.tensor.matmul(ctx_sum[:, h, :], pt_hi[:, h, :], v_hi[:, vi, h, :], start=True, stop=False)
                        nc.tensor.matmul(ctx_sum[:, h, :], pt_lo[:, h, :], v_hi[:, vi, h, :], start=False, stop=False)
                        last = nc.tensor.matmul(ctx_sum[:, h, 0:D], pt_hi[:, h, :], v_lo[:, vi, h, 0:D], start=False,
                                                stop=True)
                    last.then_inc(s_pv, 1)
                if has(g - 1):
                    done(pe, s_ct_lo, g - 1)
                    if has(k):
                        done(pe, s_chunk_lo[2], k)
                    else:
                        done(pe, s_out, g - 2)
                    pairs = []
                    for c in range(C):
                        pairs += [(ct_hi[:, c, :], w_hi[:, 3, c, :]),
                                  (ct_lo[:, c, :], w_hi[:, 3, c, :]),
                                  (ct_hi[:, c, :], w_lo[:, 3, c, :])]
                    split_matmuls(proj_bank(s, 4)[:, 0:H], pairs, True, True).then_inc(s_y, 1)
                if has(g):
                    done(pe, s_context, g)
                    if has(g + HT_AHEAD):
                        done(pe, s_h_lo, g + HT_AHEAD)
                    else:
                        done(pe, s_ct_lo, g - 1)
                    for c in range(C):
                        last = nc.tensor.transpose(turn[:, c, :], context[:, c * P:(c + 1) * P], ident[:, :])
                    last.then_inc(s_turn_c, 1)

            run_slots(pe, slot)


_INS = ['x', 'adj', 'L0_gnn_Wq', 'L0_gnn_bq', 'L0_gnn_Wk', 'L0_gnn_bk', 'L0_gnn_Wv', 'L0_gnn_bv', 'L0_gnn_Wf',
        'L0_gnn_bf']
_OUTS = [((128, 128, 384), 'float32')]


def kernel(**inputs):
    import numpy as _np
    import concourse.bacc as _bacc
    from concourse import mybir as _mybir
    from concourse.bass_utils import run_bass_kernel_spmd as _run

    nc = _bacc.Bacc("TRN2", target_bir_lowering=False, num_devices=1)
    arrays, args = {}, []
    for name in _INS:
        a = _np.ascontiguousarray(inputs[name])
        arrays[f"in_{name}_dram"] = a
        args.append(nc.dram_tensor(f"in_{name}_dram", a.shape, _mybir.dt.from_np(a.dtype), kind="ExternalInput").ap())
    for i, (shape, dtype) in enumerate(_OUTS):
        dt = _mybir.dt.from_np(_np.dtype(dtype))
        args.append(nc.dram_tensor(f"out_{i}_dram", shape, dt, kind="ExternalOutput").ap())
    gnn_kernel(nc, *args)
    r = _run(nc, [arrays], core_ids=[0])
    got = tuple(r.results[0][f"out_{i}_dram"] for i in range(len(_OUTS)))
    return got[0]
```

```python
from contextlib import ExitStack

import concourse.bass as bass
from concourse import mybir

ALU = mybir.AluOpType
ACT = mybir.ActivationFunctionType
F32 = mybir.dt.float32
F16 = mybir.dt.float16
BF16 = mybir.dt.bfloat16
U8 = mybir.dt.uint8
U32 = mybir.dt.uint32
AX_X = mybir.AxisListType.X
RMAX = bass.bass_isa.ReduceOp.max

P = 128
HEADS = 6
EPS = 1e-5
NEG = -9000000000000000.0

H_UP = 4.0
W_UP = 8.0
UP = H_UP * W_UP

PROJ_AHEAD = 2
HT_AHEAD = 4
NORM_AHEAD = 6
MASK_AHEAD = 2
MIX_BEHIND = 1
OUT_BEHIND = 2
STORE_BEHIND = 4
RING = 16
UNROLL = 4


def gnn_kernel(nc: bass.Bass, x, adj, Wq, bq, Wk, bk, Wv, bv, Wf, bf, out):
    B, S, H = x.shape
    D = H // HEADS
    C = H // P
    PAIR = 2 * S
    V1 = D + 1
    assert S == P and C * P == H and B % UNROLL == 0

    x_pair = x.rearrange("(n a) t h -> n t a h", a=2)
    adj_pair = adj.rearrange("(n a) q k -> n q a k", a=2)
    out_pair = out.rearrange("(n a) t h -> n t a h", a=2)

    with ExitStack() as ctx:
        def sb(name, shape, dt):
            return ctx.enter_context(nc.sbuf_tensor(name, shape, dt))

        def psum(name, shape):
            return ctx.enter_context(nc.psum_tensor(name, shape, F32))

        def sem(name):
            return ctx.enter_context(nc.semaphore(name))

        w_raw = sb("w_raw", [P, 4, C, H], F32)
        w_hi = sb("w_hi", [P, 4, C, H], F16)
        w_lo = sb("w_lo", [P, 4, C, H], F16)
        b_raw = sb("b_raw", [P, 3, C], F32)
        b_up = sb("b_up", [P, 2, C], F32)
        bv_wide = sb("bv_wide", [P, C, P], F32)
        bf_rows = sb("bf_rows", [P, H], F32)
        out_bias = sb("out_bias", [P, H], F32)
        ident = sb("ident", [P, P], F32)
        peak = sb("peak", [P, 8], F32)
        peak_all = sb("peak_all", [P, 8], F32)
        size = sb("size", [P, 4], F32)
        pow2 = sb("pow2", [P, 4], F32)
        pow2_inv = sb("pow2_inv", [P, 4], F32)
        w_scale = sb("w_scale", [P, 4], F32)
        consts = sb("consts", [P, 8], F32)
        exponent = sb("exponent", [P, 1], F32)
        score_scale = consts[:, 0:1]
        out_scale = consts[:, 1:2]
        x_in = sb("x_in", [P, 2, 2, H], F32)
        adj_in = sb("adj_in", [P, 2, 2, S], U8)
        stats = sb("stats", [P, 4, 6], F32)
        mean_var = sb("mean_var", [P, 4, 2], F32)
        neg_mean = sb("neg_mean", [P, 4], F32)
        var_eps = sb("var_eps", [P, 4], F32)
        rstd = sb("rstd", [P, 4], F32)
        shift = sb("shift", [P, 4], F32)
        x_norm = sb("x_norm", [P, 4, H], F32)
        resid = sb("resid", [P, RING * H], F32)
        mask = sb("mask", [P, 4, C * S], F32)
        h_hi = sb("h_hi", [P, 2, C, PAIR], F16)
        h_lo = sb("h_lo", [P, 2, C, PAIR], F16)
        qk_hi = sb("qk_hi", [P, 2, 2, C, PAIR], F16)
        qk_lo = sb("qk_lo", [P, 2, 2, C, PAIR], F16)
        v_hi = sb("v_hi", [P, 4, HEADS, V1], F16)
        v_lo = sb("v_lo", [P, 4, HEADS, V1], F16)
        masked = sb("masked", [P, 2, C * S], F32)
        neg_max = sb("neg_max", [P, 2, C], F32)
        probs = sb("probs", [P, 2, C, S], F32)
        pt_hi = sb("pt_hi", [P, HEADS, S], F16)
        pt_lo = sb("pt_lo", [P, HEADS, S], F16)
        inv_sum = sb("inv_sum", [P, HEADS], F32)
        context = sb("context", [P, H], F32)
        ct_hi = sb("ct_hi", [P, C, S], F16)
        ct_lo = sb("ct_lo", [P, C, S], F16)
        y_out = sb("y_out", [P, 2, 2, H], F32)

        ps_scores = psum("ps_scores", [P, 2, 512])
        ps_pt = psum("ps_pt", [P, 2, 512])
        ps_proj = [psum(f"ps_proj{i}", [P, 512]) for i in range(2)]
        ps_ctx = psum("ps_ctx", [P, 512])
        ps_turn = psum("ps_turn", [P, 512])
        scores = ps_scores[:, :, 0:C * S].rearrange("p r (c k) -> p r c k", c=C)
        pt = ps_pt[:, :, :].rearrange("p b n -> p (b n)")[:, 0:HEADS * S].rearrange(
            "p (h k) -> p h k", h=HEADS)
        ctx_sum = ps_ctx[:, 0:HEADS * V1].rearrange("p (h d) -> p h d", h=HEADS)
        turn = ps_turn[:, 0:H].rearrange("p (c t) -> p c t", c=C)

        s_weights = [sem(f"s_weights{i}") for i in range(4)]
        s_small = sem("s_small")
        s_x = [sem(f"s_x{i}") for i in range(2)]
        s_adj = [sem(f"s_adj{i}") for i in range(2)]
        s_store = [sem(f"s_store{i}") for i in range(2)]
        s_ident = sem("s_ident")
        s_peak = sem("s_peak")
        s_peak_all = sem("s_peak_all")
        s_scale = sem("s_scale")
        s_w_hi = sem("s_w_hi")
        s_w_lo = sem("s_w_lo")
        s_bv_wide = sem("s_bv_wide")
        s_bvwf = sem("s_bvwf")
        s_out_bias = sem("s_out_bias")
        s_ones = sem("s_ones")
        s_moments = sem("s_moments")
        s_mean_var = sem("s_mean_var")
        s_stats = sem("s_stats")
        s_rstd = sem("s_rstd")
        s_shift = sem("s_shift")
        s_norm = sem("s_norm")
        s_resid = sem("s_resid")
        s_mask = sem("s_mask")
        s_turn_h = sem("s_turn_h")
        s_h_hi = sem("s_h_hi")
        s_h_lo = sem("s_h_lo")
        s_chunk = [sem(f"s_chunk{i}") for i in range(3)]
        s_chunk_hi = [sem(f"s_chunk_hi{i}") for i in range(3)]
        s_chunk_lo = [sem(f"s_chunk_lo{i}") for i in range(3)]
        s_v = sem("s_v")
        s_v_hi = sem("s_v_hi")
        s_v_lo = sem("s_v_lo")
        s_scores = sem("s_scores")
        s_masked = sem("s_masked")
        s_max = sem("s_max")
        s_exp = sem("s_exp")
        s_turn_p = sem("s_turn_p")
        s_pt_hi = sem("s_pt_hi")
        s_pt_lo = sem("s_pt_lo")
        s_pv = sem("s_pv")
        s_inv = sem("s_inv")
        s_context = sem("s_context")
        s_turn_c = sem("s_turn_c")
        s_ct_hi = sem("s_ct_hi")
        s_ct_lo = sem("s_ct_lo")
        s_y = sem("s_y")
        s_out = sem("s_out")

        def done(eng, semaphore, k):
            if not isinstance(k, int) or k >= 0:
                eng.wait_ge(semaphore, k + 1)

        def landed(eng, semaphore, turn_no):
            if not isinstance(turn_no, int) or turn_no >= 0:
                eng.wait_ge(semaphore, turn_no * 16 + 16)

        def has(g):
            return not isinstance(g, int) or 0 <= g < B

        FIRST = -NORM_AHEAD
        LOOP_FROM, LOOP_TO = 2 * UNROLL, B - 3 * UNROLL
        LAST = B - 2 + STORE_BEHIND

        def first_slots(slot, start, end):
            for g in range(start, end):
                slot(g, g % UNROLL)

        def run_slots(eng, slot, start):
            first_slots(slot, start, LOOP_FROM)
            with eng.Fori(LOOP_FROM, LOOP_TO - UNROLL + 1, UNROLL) as g0:
                for s in range(UNROLL):
                    slot(g0 + s if s else g0, s)
            for g in range(LOOP_TO, LAST + 1):
                slot(g, g % UNROLL)

        def at(s, ahead):
            return (s + ahead) % 4

        def pair_of(s, ahead):
            return at(s, ahead) // 2, at(s, ahead) % 2

        def proj_bank(s, use):
            return ps_proj[(s + use) % 2]

        def split_matmuls(o, pairs, start, stop):
            for i, (w, m) in enumerate(pairs):
                last = nc.tensor.matmul(o, w, m, start=start and i == 0, stop=stop and i == len(pairs) - 1)
            return last

        block = ctx.enter_context(nc.Block())

        @block.sync
        def _(sp):
            def load_x(n, parity):
                sp.dma_start(x_in[:, parity, :, :], x_pair[n]).then_inc(s_x[parity], 16)

            def load_adj(n, parity):
                sp.dma_start(adj_in[:, parity, :, :], adj_pair[n]).then_inc(s_adj[parity], 16)

            load_x(0, 0)
            for i, w in ((1, Wk), (3, Wf)):
                sp.dma_start(w_raw[:, i, :, :], w.rearrange("(c p) n -> p c n", p=P)).then_inc(s_weights[i], 16)
            load_x(1, 1)
            for n in range(2):
                load_adj(n, n)

            def slot(g, s):
                if s % 2:
                    return
                n = g // 2 if isinstance(g, int) else g >> 1
                if has(g - STORE_BEHIND):
                    parity, _ = pair_of(s, -STORE_BEHIND)
                    done(sp, s_out, g - STORE_BEHIND + 1)
                    sp.dma_start(out_pair[n - STORE_BEHIND // 2], y_out[:, parity, :, :]).then_inc(s_store[parity], 16)
                if has(g + MASK_AHEAD + 4) and has(g + MASK_AHEAD):
                    parity, _ = pair_of(s, MASK_AHEAD)
                    done(sp, s_mask, g + MASK_AHEAD + 1)
                    load_adj(n + MASK_AHEAD // 2 + 2, parity)
                if has(g + NORM_AHEAD + 4):
                    parity, _ = pair_of(s, NORM_AHEAD)
                    done(sp, s_norm, g + NORM_AHEAD + 1)
                    done(sp, s_resid, g + NORM_AHEAD + 1)
                    load_x(n + NORM_AHEAD // 2 + 2, parity)

            run_slots(sp, slot, FIRST)
            for parity in range(2):
                sp.wait_ge(s_store[parity], 16 * (B // 4))

        @block.gpsimd
        def _(pool):
            nc.gpsimd.memset(exponent[:, :], -0.5).then_inc(s_ident, 1)
            nc.gpsimd.memset(ident[:, :], 0.0).then_inc(s_ident, 1)
            pool.wait_ge(s_ident, 2)
            nc.gpsimd.affine_select(out=ident[:, :], in_=ident[:, :], compare_op=ALU.not_equal, fill=1.0,
                                    base=0, pattern=[[-1, P]], channel_multiplier=1).then_inc(s_ident, 1)
            nc.gpsimd.memset(v_hi[:, :, :, D:V1], 1.0).then_inc(s_ones, 1)

            def residual(m, s, ahead):
                parity, a = pair_of(s, ahead)
                place = (m % RING if isinstance(m, int) else m & (RING - 1)) * H
                nc.gpsimd.tensor_tensor(resid[:, bass.ds(place, H)], x_in[:, parity, a, :], out_bias[:, :],
                                        ALU.add).then_inc(s_resid, 1)

            def slot(g, s):
                if g == FIRST + 4 if isinstance(g, int) else False:
                    pool.wait_ge(s_out_bias, 1)
                    for m in range(4):
                        residual(m, m, 0)
                m = g + NORM_AHEAD
                if has(m):
                    i = at(s, NORM_AHEAD)
                    parity, a = pair_of(s, NORM_AHEAD)
                    col = slice(i, i + 1)
                    done(pool, s_stats, m)
                    done(pool, s_norm, m - 4)
                    nc.gpsimd.tensor_tensor(rstd[:, col], var_eps[:, col], exponent[:, :], ALU.pow).then_inc(s_rstd, 1)
                    done(pool, s_rstd, m)
                    nc.gpsimd.tensor_tensor(shift[:, col], neg_mean[:, col], rstd[:, col], ALU.mult).then_inc(s_shift, 1)
                    done(pool, s_turn_h, m - 4)
                    done(pool, s_shift, m)
                k = g + MASK_AHEAD
                if has(k):
                    mask_parity, mask_a = pair_of(s, MASK_AHEAD)
                    landed(pool, s_adj[mask_parity], k // 4 if isinstance(k, int) else k >> 2)
                    done(pool, s_masked, k - 4)
                if has(m) and g >= FIRST + 4 if isinstance(g, int) else True:
                    residual(m, s, NORM_AHEAD)
                if has(m):
                    nc.gpsimd.tensor_scalar(x_norm[:, i, :], x_in[:, parity, a, :], rstd[:, col], shift[:, col],
                                            ALU.mult, ALU.add).then_inc(s_norm, 1)
                if has(k):
                    nc.gpsimd.tensor_scalar(mask[:, at(s, MASK_AHEAD), :].rearrange("p (c k) -> p c k", c=C),
                                            adj_in[:, mask_parity, mask_a, :].unsqueeze(1).broadcast_to([P, C, S]),
                                            -NEG, NEG, ALU.mult, ALU.add).then_inc(s_mask, 1)

            first_slots(slot, FIRST, FIRST + 2)
            pool.wait_ge(s_peak, 7)
            nc.gpsimd.partition_all_reduce(peak_all[:, :], peak[:, :], P, RMAX).then_inc(s_peak_all, 1)
            run_slots(pool, slot, FIRST + 2)

        @block.scalar
        def _(act):
            for i, w in ((0, Wq), (2, Wv)):
                act.dma_start(w_raw[:, i, :, :], w.rearrange("(c p) n -> p c n", p=P)).then_inc(s_weights[i], 16)
            for i, b in enumerate((bq, bk, bv)):
                act.dma_start(b_raw[:, i, :], b.rearrange("(c p) -> p c", p=P),
                              allow_slow_non_contiguous=True).then_inc(s_small, 16)
            act.dma_start(bf_rows[:, :], bf.rearrange("(a n) -> a n", a=1).broadcast_to([P, H])).then_inc(s_small, 16)
            act.wait_ge(s_small, 64)
            nc.scalar.copy(bv_wide[:, :, :], b_raw[:, 2, :].unsqueeze(2).broadcast_to([P, C, P])).then_inc(s_bv_wide, 1)

            def slot(g, s):
                k = g + PROJ_AHEAD
                parity, a = pair_of(s, PROJ_AHEAD)
                mix = g - MIX_BEHIND

                def chunk(c):
                    if has(k):
                        done(act, s_chunk[c], k)
                        nc.scalar.activation(qk_hi[:, parity, a, c, :], proj_bank(s, c)[:, 0:PAIR], ACT.Identity,
                                             bias=b_up[:, a, c:c + 1]).then_inc(s_chunk_hi[c], 1)

                if has(mix):
                    done(act, s_turn_p, mix)
                    nc.scalar.activation(pt_hi[:, :, :], pt, ACT.Copy).then_inc(s_pt_hi, 1)
                chunk(0)
                chunk(1)
                if has(g + HT_AHEAD):
                    hp, ha = pair_of(s, HT_AHEAD)
                    done(act, s_turn_h, g + HT_AHEAD)
                    nc.scalar.activation(h_hi[:, hp, :, ha * S:(ha + 1) * S], turn, ACT.Relu).then_inc(s_h_hi, 1)
                chunk(2)
                if has(g):
                    done(act, s_max, g)
                    for r in range(2):
                        for c in range(C):
                            last = nc.scalar.activation(probs[:, r, c, :], masked[:, r, c * S:(c + 1) * S], ACT.Exp,
                                                        bias=neg_max[:, r, c:c + 1])
                    last.then_inc(s_exp, 1)
                if has(k):
                    done(act, s_v, k)
                    if isinstance(k, int) and k == 0:
                        act.wait_ge(s_ones, 1)
                    nc.scalar.activation(v_hi[:, at(s, PROJ_AHEAD), :, 0:D],
                                         proj_bank(s, 3)[:, 0:H].rearrange("p (h d) -> p h d", h=HEADS),
                                         ACT.Copy).then_inc(s_v_hi, 1)
                if has(mix):
                    done(act, s_turn_c, mix)
                    nc.scalar.activation(ct_hi[:, :, :], turn, ACT.Copy).then_inc(s_ct_hi, 1)

            act.wait_ge(s_scale, 4)
            for i in range(4):
                nc.scalar.activation(w_hi[:, i, :, :], w_raw[:, i, :, :], ACT.Copy,
                                     scale=w_scale[:, i:i + 1]).then_inc(s_w_hi, 1)
                if i == 0:
                    first_slots(slot, FIRST, FIRST + 4)
            act.wait_ge(s_scale, 6)
            run_slots(act, slot, FIRST + 4)

        @block.vector
        def _(dve):
            def slot(g, s):
                k = g + PROJ_AHEAD
                parity, a = pair_of(s, PROJ_AHEAD)
                mix = g - MIX_BEHIND

                def chunk(c):
                    if has(k):
                        done(dve, s_chunk_hi[c], k)
                        nc.vector.scalar_tensor_tensor(qk_lo[:, parity, a, c, :], proj_bank(s, c)[:, 0:PAIR],
                                                       b_up[:, a, c:c + 1], qk_hi[:, parity, a, c, :], ALU.add,
                                                       ALU.subtract).then_inc(s_chunk_lo[c], 1)

                m = g + NORM_AHEAD
                if has(m):
                    i = at(s, NORM_AHEAD)
                    xp, xa = pair_of(s, NORM_AHEAD)
                    landed(dve, s_x[xp], m // 4 if isinstance(m, int) else m >> 2)
                    nc.vector.bn_stats(stats[:, i, :], x_in[:, xp, xa, :]).then_inc(s_moments, 1)
                if has(mix):
                    done(dve, s_pt_hi, mix)
                    nc.vector.tensor_tensor(pt_lo[:, :, :], pt, pt_hi[:, :, :], ALU.subtract).then_inc(s_pt_lo, 1)
                chunk(0)
                if has(g):
                    done(dve, s_scores, g)
                    done(dve, s_mask, g)
                    done(dve, s_exp, g - 1)
                    nc.vector.scalar_tensor_tensor(masked[:, :, :], ps_scores[:, :, 0:C * S], score_scale,
                                                   mask[:, at(s, 0), :].unsqueeze(1).broadcast_to([P, 2, C * S]),
                                                   ALU.mult, ALU.add).then_inc(s_masked, 1)
                chunk(1)
                if has(g):
                    done(dve, s_masked, g)
                    nc.vector.tensor_reduce(neg_max[:, :, :], masked[:, :, :].rearrange("p r (c k) -> p r c k", c=C), AX_X, ALU.max,
                                            negate=True).then_inc(s_max, 1)
                chunk(2)
                if has(g + HT_AHEAD):
                    hp, ha = pair_of(s, HT_AHEAD)
                    part = slice(ha * S, (ha + 1) * S)
                    done(dve, s_h_hi, g + HT_AHEAD)
                    nc.vector.scalar_tensor_tensor(h_lo[:, hp, :, part], turn, 0.0, h_hi[:, hp, :, part], ALU.max,
                                                   ALU.subtract).then_inc(s_h_lo, 1)
                if has(m):
                    done(dve, s_moments, m)
                if has(mix):
                    done(dve, s_pv, mix)
                    nc.vector.reciprocal(inv_sum[:, :], ctx_sum[:, :, D]).then_inc(s_inv, 1)
                    done(dve, s_inv, mix)
                    nc.vector.tensor_tensor(context[:, :].rearrange("p (h d) -> p h d", h=HEADS), ctx_sum[:, :, 0:D],
                                            inv_sum[:, :].unsqueeze(2).broadcast_to([P, HEADS, D]),
                                            ALU.mult).then_inc(s_context, 1)
                if has(m):
                    nc.vector.bn_aggr(mean_var[:, i, :], stats[:, i, :]).then_inc(s_mean_var, 1)
                if has(k):
                    done(dve, s_v_hi, k)
                    vi = at(s, PROJ_AHEAD)
                    nc.vector.tensor_tensor(v_lo[:, vi, :, 0:D],
                                            proj_bank(s, 3)[:, 0:H].rearrange("p (h d) -> p h d", h=HEADS),
                                            v_hi[:, vi, :, 0:D], ALU.subtract).then_inc(s_v_lo, 1)
                if has(m):
                    done(dve, s_shift, m - 4)
                    done(dve, s_mean_var, m)
                    nc.vector.tensor_scalar(var_eps[:, i:i + 1], mean_var[:, i, 1:2], H_UP ** -2, EPS * H_UP ** -2,
                                            ALU.mult, ALU.add)
                    nc.vector.tensor_scalar(neg_mean[:, i:i + 1], mean_var[:, i, 0:1], -1.0, None,
                                            ALU.mult).then_inc(s_stats, 1)
                y = g - OUT_BEHIND
                if has(y):
                    op, oa = pair_of(s, -OUT_BEHIND)
                    done(dve, s_y, y)
                    done(dve, s_resid, y)
                    landed(dve, s_store[op], y // 4 - 1 if isinstance(y, int) else (y >> 2) - 1)
                    place = (y % RING if isinstance(y, int) else y & (RING - 1)) * H
                    nc.vector.scalar_tensor_tensor(y_out[:, op, oa, :], proj_bank(s, 4)[:, 0:H], out_scale,
                                                   resid[:, bass.ds(place, H)], ALU.mult, ALU.add).then_inc(s_out, 1)
                if has(mix):
                    done(dve, s_ct_hi, mix)
                    nc.vector.tensor_tensor(ct_lo[:, :, :], turn, ct_hi[:, :, :], ALU.subtract).then_inc(s_ct_lo, 1)

            first_slots(slot, FIRST, FIRST + 2)
            nc.vector.memset(peak[:, 6:8], 0.0).then_inc(s_peak, 1)
            dve.wait_ge(s_small, 64)
            nc.vector.tensor_reduce(peak[:, 4:6], b_raw[:, 0:2, :], AX_X, ALU.max,
                                    apply_absolute_value=True).then_inc(s_peak, 1)
            dve.wait_ge(s_peak, 2)
            nc.vector.tensor_scalar(peak[:, 4:6], peak[:, 4:6], 1.0 / P, None, ALU.mult).then_inc(s_peak, 1)
            for i in range(4):
                dve.wait_ge(s_weights[i], 16)
                nc.vector.tensor_reduce(peak[:, i:i + 1], w_raw[:, i, :, :].rearrange("p c n -> p (c n)"), AX_X,
                                        ALU.max, apply_absolute_value=True).then_inc(s_peak, 1)
            dve.wait_ge(s_peak_all, 1)
            nc.vector.tensor_tensor(peak_all[:, 0:2], peak_all[:, 0:2], peak_all[:, 4:6], ALU.max).then_inc(s_scale, 1)
            dve.wait_ge(s_scale, 1)
            nc.vector.tensor_scalar(size[:, :], peak_all[:, 0:4], 2.0 ** -30, 2.0 ** 40, ALU.max, ALU.min).then_inc(s_scale, 1)
            dve.wait_ge(s_scale, 2)
            nc.vector.tensor_scalar(pow2[:, :].bitcast(U32), size[:, :].bitcast(U32), 0x7F800000, None,
                                    ALU.bitwise_and).then_inc(s_scale, 1)
            dve.wait_ge(s_scale, 3)
            nc.vector.reciprocal(pow2_inv[:, :], pow2[:, :]).then_inc(s_peak, 1)
            dve.wait_ge(s_peak, 8)
            nc.vector.tensor_scalar(w_scale[:, :], pow2_inv[:, :], W_UP, None, ALU.mult).then_inc(s_scale, 1)
            nc.vector.scalar_tensor_tensor(score_scale, pow2[:, 0:1], 1.0 / (UP * UP * D ** 0.5), pow2[:, 1:2],
                                           ALU.mult, ALU.mult).then_inc(s_peak, 1)
            nc.vector.scalar_tensor_tensor(out_scale, pow2[:, 2:3], 1.0 / (UP * W_UP), pow2[:, 3:4],
                                           ALU.mult, ALU.mult).then_inc(s_peak, 1)
            dve.wait_ge(s_peak, 10)
            for i in range(2):
                nc.vector.tensor_scalar(b_up[:, i, :], b_raw[:, i, :], pow2_inv[:, i:i + 1], UP, ALU.mult,
                                        ALU.mult).then_inc(s_scale, 1)
            dve.wait_ge(s_bvwf, 1)
            nc.vector.tensor_tensor(out_bias[:, :], ps_ctx[:, 0:H], bf_rows[:, :], ALU.add).then_inc(s_out_bias, 1)
            for i in range(4):
                dve.wait_ge(s_w_hi, i + 1)
                nc.vector.scalar_tensor_tensor(w_lo[:, i, :, :].rearrange("p c n -> p (c n)"),
                                               w_raw[:, i, :, :].rearrange("p c n -> p (c n)"), w_scale[:, i:i + 1],
                                               w_hi[:, i, :, :].rearrange("p c n -> p (c n)"), ALU.mult,
                                               ALU.subtract).then_inc(s_w_lo, 1)
                if i == 0:
                    first_slots(slot, FIRST + 2, FIRST + 4)
            run_slots(dve, slot, FIRST + 4)

        @block.tensor
        def _(pe):
            pe.wait_ge(s_weights[3], 16)
            pe.wait_ge(s_bv_wide, 1)
            for c in range(C):
                last = nc.tensor.matmul(ps_ctx[:, 0:H], bv_wide[:, c, :], w_raw[:, 3, c, :], start=(c == 0),
                                        stop=(c == C - 1))
            last.then_inc(s_bvwf, 1)
            pe.wait_ge(s_ident, 3)

            def slot(g, s):
                k = g + PROJ_AHEAD
                parity, a = pair_of(s, PROJ_AHEAD)
                cur, half = pair_of(s, 0)
                mix = g - MIX_BEHIND
                y = g - OUT_BEHIND

                def weights_ready(matrix):
                    if isinstance(g, int) and g <= OUT_BEHIND:
                        pe.wait_ge(s_w_lo, matrix + 1)

                def chunk(c):
                    feats = slice(c * P, (c + 1) * P)
                    pairs = []
                    for i in range(C):
                        pairs += [(w_hi[:, a, i, feats], h_hi[:, parity, i, :]),
                                  (w_hi[:, a, i, feats], h_lo[:, parity, i, :]),
                                  (w_lo[:, a, i, feats], h_hi[:, parity, i, :])]
                    weights_ready(a)
                    split_matmuls(proj_bank(s, c)[:, 0:PAIR], pairs, True, True).then_inc(s_chunk[c], 1)

                if has(mix):
                    done(pe, s_exp, mix)
                    done(pe, s_pt_lo, mix - 1)
                    for h in range(HEADS):
                        last = nc.tensor.transpose(pt[:, h, :], probs[:, h % 2, h // 2, :], ident[:, :])
                    last.then_inc(s_turn_p, 1)
                if has(k):
                    if a == 0:
                        done(pe, s_h_lo, k + 1)
                    done(pe, s_v_lo, k - 1)
                    chunk(0)
                if has(g):
                    if half == 0:
                        done(pe, s_chunk_lo[2], g + 1)
                    done(pe, s_masked, g - 1)
                    tok = slice(half * S, (half + 1) * S)
                    for c in range(C):
                        for i, (q, kk) in enumerate(((qk_hi, qk_hi), (qk_lo, qk_hi), (qk_hi, qk_lo))):
                            for r in range(2):
                                rows = slice(r * D, (r + 1) * D)
                                last = nc.tensor.matmul(scores[:, r, c, :], q[rows, cur, 0, c, tok],
                                                        kk[rows, cur, 1, c, tok], start=(i == 0), stop=(i == 2))
                    last.then_inc(s_scores, 1)
                if has(k):
                    done(pe, s_out, y - 1)
                    chunk(1)
                if has(g + HT_AHEAD):
                    done(pe, s_norm, g + HT_AHEAD)
                    done(pe, s_ct_lo, mix - 1)
                    if isinstance(g, int) and not has(mix - 1):
                        done(pe, s_h_lo, g + HT_AHEAD - 1)
                    for c in range(C):
                        last = nc.tensor.transpose(turn[:, c, :], x_norm[:, at(s, HT_AHEAD), c * P:(c + 1) * P],
                                                   ident[:, :])
                    last.then_inc(s_turn_h, 1)
                if has(k):
                    done(pe, s_chunk_lo[0], k)
                    chunk(2)
                if has(mix):
                    done(pe, s_pt_lo, mix)
                    done(pe, s_v_lo, mix)
                    done(pe, s_context, mix - 1)
                    vi = at(s, -MIX_BEHIND)
                    for h in range(HEADS):
                        nc.tensor.matmul(ctx_sum[:, h, :], pt_hi[:, h, :], v_hi[:, vi, h, :], start=True, stop=False)
                        nc.tensor.matmul(ctx_sum[:, h, :], pt_lo[:, h, :], v_hi[:, vi, h, :], start=False, stop=False)
                        last = nc.tensor.matmul(ctx_sum[:, h, 0:D], pt_hi[:, h, :], v_lo[:, vi, h, 0:D], start=False,
                                                stop=True)
                    last.then_inc(s_pv, 1)
                if has(k):
                    done(pe, s_chunk_lo[1], k)
                    tok = slice(a * S, (a + 1) * S)
                    pairs = []
                    for i in range(C):
                        pairs += [(h_hi[:, parity, i, tok], w_hi[:, 2, i, :]),
                                  (h_lo[:, parity, i, tok], w_hi[:, 2, i, :]),
                                  (h_hi[:, parity, i, tok], w_lo[:, 2, i, :])]
                    weights_ready(2)
                    split_matmuls(proj_bank(s, 3)[:, 0:H], pairs, True, True).then_inc(s_v, 1)
                if has(y):
                    done(pe, s_ct_lo, y)
                    if has(k):
                        done(pe, s_chunk_lo[2], k)
                    else:
                        done(pe, s_out, y - 1)
                    pairs = []
                    for c in range(C):
                        pairs += [(ct_hi[:, c, :], w_hi[:, 3, c, :]),
                                  (ct_lo[:, c, :], w_hi[:, 3, c, :]),
                                  (ct_hi[:, c, :], w_lo[:, 3, c, :])]
                    weights_ready(3)
                    split_matmuls(proj_bank(s, 4)[:, 0:H], pairs, True, True).then_inc(s_y, 1)
                if has(mix):
                    done(pe, s_context, mix)
                    if has(g + HT_AHEAD):
                        done(pe, s_h_lo, g + HT_AHEAD)
                    else:
                        done(pe, s_ct_lo, mix - 1)
                    for c in range(C):
                        last = nc.tensor.transpose(turn[:, c, :], context[:, c * P:(c + 1) * P], ident[:, :])
                    last.then_inc(s_turn_c, 1)

            run_slots(pe, slot, FIRST)


_INS = ['x', 'adj', 'L0_gnn_Wq', 'L0_gnn_bq', 'L0_gnn_Wk', 'L0_gnn_bk', 'L0_gnn_Wv', 'L0_gnn_bv', 'L0_gnn_Wf',
        'L0_gnn_bf']
_OUTS = [((128, 128, 384), 'float32')]


def kernel(**inputs):
    import numpy as _np
    import concourse.bacc as _bacc
    from concourse import mybir as _mybir
    from concourse.bass_utils import run_bass_kernel_spmd as _run

    nc = _bacc.Bacc("TRN2", target_bir_lowering=False, num_devices=1)
    arrays, args = {}, []
    for name in _INS:
        a = _np.ascontiguousarray(inputs[name])
        arrays[f"in_{name}_dram"] = a
        args.append(nc.dram_tensor(f"in_{name}_dram", a.shape, _mybir.dt.from_np(a.dtype), kind="ExternalInput").ap())
    for i, (shape, dtype) in enumerate(_OUTS):
        dt = _mybir.dt.from_np(_np.dtype(dtype))
        args.append(nc.dram_tensor(f"out_{i}_dram", shape, dt, kind="ExternalOutput").ap())
    gnn_kernel(nc, *args)
    r = _run(nc, [arrays], core_ids=[0])
    got = tuple(r.results[0][f"out_{i}_dram"] for i in range(len(_OUTS)))
    return got[0]
```

```python
from contextlib import ExitStack

import concourse.bass as bass
from concourse import mybir

ALU = mybir.AluOpType
ACT = mybir.ActivationFunctionType
F32 = mybir.dt.float32
F16 = mybir.dt.float16
BF16 = mybir.dt.bfloat16
U8 = mybir.dt.uint8
U32 = mybir.dt.uint32
AX_X = mybir.AxisListType.X
RMAX = bass.bass_isa.ReduceOp.max

P = 128
HEADS = 6
EPS = 1e-5
NEG = -9000000000000000.0

H_UP = 4.0
W_UP = 8.0
UP = H_UP * W_UP

PROJ_AHEAD = 2
HT_AHEAD = 4
NORM_AHEAD = 6
MASK_AHEAD = 2
MIX_BEHIND = 1
OUT_BEHIND = 2
STORE_BEHIND = 4
RING = 16
UNROLL = 4


def gnn_kernel(nc: bass.Bass, x, adj, Wq, bq, Wk, bk, Wv, bv, Wf, bf, out):
    B, S, H = x.shape
    D = H // HEADS
    C = H // P
    PAIR = 2 * S
    V1 = D + 1
    assert S == P and C * P == H and B % UNROLL == 0

    x_pair = x.rearrange("(n a) t h -> n t a h", a=2)
    adj_pair = adj.rearrange("(n a) q k -> n q a k", a=2)
    out_pair = out.rearrange("(n a) t h -> n t a h", a=2)

    with ExitStack() as ctx:
        def sb(name, shape, dt):
            return ctx.enter_context(nc.sbuf_tensor(name, shape, dt))

        def psum(name, shape):
            return ctx.enter_context(nc.psum_tensor(name, shape, F32))

        def sem(name):
            return ctx.enter_context(nc.semaphore(name))

        w_raw = sb("w_raw", [P, 4, C, H], F32)
        w_hi = sb("w_hi", [P, 4, C, H], F16)
        w_lo = sb("w_lo", [P, 4, C, H], F16)
        b_raw = sb("b_raw", [P, 3, C], F32)
        b_up = sb("b_up", [P, 2, C], F32)
        bv_wide = sb("bv_wide", [P, C, P], F32)
        bf_rows = sb("bf_rows", [P, H], F32)
        out_bias = sb("out_bias", [P, H], F32)
        ident = sb("ident", [P, P], F32)
        peak_qk = sb("peak_qk", [P, 2, 2], F32)
        peak_vf = sb("peak_vf", [P, 2], F32)
        peak_qk_all = sb("peak_qk_all", [P, 2, 2], F32)
        peak_vf_all = sb("peak_vf_all", [P, 2], F32)
        size = sb("size", [P, 4], F32)
        pow2 = sb("pow2", [P, 4], F32)
        pow2_inv = sb("pow2_inv", [P, 4], F32)
        w_scale = sb("w_scale", [P, 4], F32)
        consts = sb("consts", [P, 8], F32)
        exponent = sb("exponent", [P, 1], F32)
        score_scale = consts[:, 0:1]
        out_scale = consts[:, 1:2]
        x_in = sb("x_in", [P, 2, 2, H], F32)
        adj_in = sb("adj_in", [P, 2, 2, S], U8)
        stats = sb("stats", [P, 4, 6], F32)
        mean_var = sb("mean_var", [P, 4, 2], F32)
        neg_mean = sb("neg_mean", [P, 4], F32)
        var_eps = sb("var_eps", [P, 4], F32)
        rstd = sb("rstd", [P, 4], F32)
        shift = sb("shift", [P, 4], F32)
        x_norm = sb("x_norm", [P, 4, H], F32)
        resid = sb("resid", [P, RING * H], F32)
        mask = sb("mask", [P, 4, C * S], F32)
        h_hi = sb("h_hi", [P, 2, C, PAIR], F16)
        h_lo = sb("h_lo", [P, 2, C, PAIR], F16)
        qk_hi = sb("qk_hi", [P, 2, 2, C, PAIR], F16)
        qk_lo = sb("qk_lo", [P, 2, 2, C, PAIR], F16)
        v_hi = sb("v_hi", [P, 4, HEADS, V1], F16)
        v_lo = sb("v_lo", [P, 4, HEADS, V1], F16)
        masked = sb("masked", [P, 2, C * S], F32)
        neg_max = sb("neg_max", [P, 2, C], F32)
        probs = sb("probs", [P, 2, C, S], F32)
        pt_hi = sb("pt_hi", [P, HEADS, S], F16)
        pt_lo = sb("pt_lo", [P, HEADS, S], F16)
        inv_sum = sb("inv_sum", [P, HEADS], F32)
        context = sb("context", [P, H], F32)
        ct_hi = sb("ct_hi", [P, C, S], F16)
        ct_lo = sb("ct_lo", [P, C, S], F16)
        y_out = sb("y_out", [P, 2, 2, H], F32)

        ps_scores = psum("ps_scores", [P, 2, 512])
        ps_pt = psum("ps_pt", [P, 2, 512])
        ps_proj = [psum(f"ps_proj{i}", [P, 512]) for i in range(2)]
        ps_ctx = psum("ps_ctx", [P, 512])
        ps_turn = psum("ps_turn", [P, 512])
        scores = ps_scores[:, :, 0:C * S].rearrange("p r (c k) -> p r c k", c=C)
        pt = ps_pt[:, :, :].rearrange("p b n -> p (b n)")[:, 0:HEADS * S].rearrange(
            "p (h k) -> p h k", h=HEADS)
        ctx_sum = ps_ctx[:, 0:HEADS * V1].rearrange("p (h d) -> p h d", h=HEADS)
        turn = ps_turn[:, 0:H].rearrange("p (c t) -> p c t", c=C)

        s_weights = [sem(f"s_weights{i}") for i in range(4)]
        s_bqk = sem("s_bqk")
        s_bv = sem("s_bv")
        s_bf = sem("s_bf")
        s_kept = sem("s_kept")
        s_x = [sem(f"s_x{i}") for i in range(2)]
        s_adj = [sem(f"s_adj{i}") for i in range(2)]
        s_store = [sem(f"s_store{i}") for i in range(2)]
        s_ident = sem("s_ident")
        s_peak = sem("s_peak")
        s_peak_all = sem("s_peak_all")
        s_scale = sem("s_scale")
        s_consts = sem("s_consts")
        s_w_scale = sem("s_w_scale")
        s_b_up = sem("s_b_up")
        s_w_hi = [sem(f"s_w_hi{i}") for i in range(4)]
        s_w_lo = [sem(f"s_w_lo{i}") for i in range(4)]
        s_bv_wide = sem("s_bv_wide")
        s_bvwf = sem("s_bvwf")
        s_out_bias = sem("s_out_bias")
        s_ones = sem("s_ones")
        s_moments = sem("s_moments")
        s_mean_var = sem("s_mean_var")
        s_stats = sem("s_stats")
        s_rstd = sem("s_rstd")
        s_shift = sem("s_shift")
        s_norm = sem("s_norm")
        s_resid = sem("s_resid")
        s_mask = sem("s_mask")
        s_turn_h = sem("s_turn_h")
        s_h_hi = sem("s_h_hi")
        s_h_lo = sem("s_h_lo")
        s_chunk = [sem(f"s_chunk{i}") for i in range(3)]
        s_chunk_hi = [sem(f"s_chunk_hi{i}") for i in range(3)]
        s_chunk_lo = [sem(f"s_chunk_lo{i}") for i in range(3)]
        s_v = sem("s_v")
        s_v_hi = sem("s_v_hi")
        s_v_lo = sem("s_v_lo")
        s_scores = sem("s_scores")
        s_masked = sem("s_masked")
        s_max = sem("s_max")
        s_exp = sem("s_exp")
        s_turn_p = sem("s_turn_p")
        s_pt_hi = sem("s_pt_hi")
        s_pt_lo = sem("s_pt_lo")
        s_pv = sem("s_pv")
        s_inv = sem("s_inv")
        s_context = sem("s_context")
        s_turn_c = sem("s_turn_c")
        s_ct_hi = sem("s_ct_hi")
        s_ct_lo = sem("s_ct_lo")
        s_y = sem("s_y")
        s_out = sem("s_out")

        def done(eng, semaphore, k):
            if not isinstance(k, int) or k >= 0:
                eng.wait_ge(semaphore, k + 1)

        def landed(eng, semaphore, turn_no):
            if not isinstance(turn_no, int) or turn_no >= 0:
                eng.wait_ge(semaphore, turn_no * 16 + 16)

        def has(g):
            return not isinstance(g, int) or 0 <= g < B

        FIRST = -NORM_AHEAD
        EARLY = 4
        LOOP_FROM, LOOP_TO = 2 * UNROLL, B - 3 * UNROLL
        LAST = B - 2 + STORE_BEHIND

        def first_slots(slot, start, end):
            for g in range(start, end):
                slot(g, g % UNROLL)

        def run_slots(eng, slot, start):
            first_slots(slot, start, LOOP_FROM)
            with eng.Fori(LOOP_FROM, LOOP_TO - UNROLL + 1, UNROLL) as g0:
                for s in range(UNROLL):
                    slot(g0 + s if s else g0, s)
            for g in range(LOOP_TO, LAST + 1):
                slot(g, g % UNROLL)

        def at(s, ahead):
            return (s + ahead) % 4

        def pair_of(s, ahead):
            return at(s, ahead) // 2, at(s, ahead) % 2

        def proj_bank(s, use):
            return ps_proj[(s + use) % 2]

        def usual(g):
            return not isinstance(g, int) or 0 <= g < B - 2

        def pulled(g):
            return isinstance(g, int) and B - 2 <= g < B

        def split_matmuls(o, pairs, start, stop):
            for i, (w, m) in enumerate(pairs):
                last = nc.tensor.matmul(o, w, m, start=start and i == 0, stop=stop and i == len(pairs) - 1)
            return last

        block = ctx.enter_context(nc.Block())

        @block.sync
        def _(sp):
            def load_x(n, parity):
                sp.dma_start(x_in[:, parity, :, :], x_pair[n]).then_inc(s_x[parity], 16)

            def load_w(i, w):
                sp.dma_start(w_raw[:, i, :, :], w.rearrange("(c p) n -> p c n", p=P)).then_inc(s_weights[i], 16)

            def load_adj(n, parity):
                sp.dma_start(adj_in[:, parity, :, :], adj_pair[n]).then_inc(s_adj[parity], 16)

            load_x(0, 0)
            load_x(1, 1)
            load_w(0, Wq)
            load_w(2, Wv)
            for n in range(2):
                load_adj(n, n)

            def slot(g, s):
                if s % 2:
                    return
                n = g // 2 if isinstance(g, int) else g >> 1
                if has(g - STORE_BEHIND):
                    parity, _ = pair_of(s, -STORE_BEHIND)
                    done(sp, s_out, g - STORE_BEHIND + 1)
                    sp.dma_start(out_pair[n - STORE_BEHIND // 2], y_out[:, parity, :, :]).then_inc(s_store[parity], 16)
                if has(g + MASK_AHEAD + 4) and has(g + MASK_AHEAD):
                    parity, _ = pair_of(s, MASK_AHEAD)
                    done(sp, s_mask, g + MASK_AHEAD + 1)
                    load_adj(n + MASK_AHEAD // 2 + 2, parity)
                if has(g + NORM_AHEAD + 4):
                    parity, _ = pair_of(s, NORM_AHEAD)
                    done(sp, s_norm, g + NORM_AHEAD + 1)
                    early = isinstance(g, int) and g < FIRST + EARLY
                    done(sp, s_kept if early else s_resid, g + NORM_AHEAD + 1)
                    load_x(n + NORM_AHEAD // 2 + 2, parity)

            run_slots(sp, slot, FIRST)
            for parity in range(2):
                sp.wait_ge(s_store[parity], 16 * (B // 4))

        @block.gpsimd
        def _(pool):
            pool.dma_start(b_raw[:, 2, :], bv.rearrange("(c p) -> p c", p=P),
                           allow_slow_non_contiguous=True).then_inc(s_bv, 16)
            pool.dma_start(bf_rows[:, :], bf.rearrange("(a n) -> a n", a=1).broadcast_to([P, H])).then_inc(s_bf, 16)
            nc.gpsimd.memset(exponent[:, :], -0.5).then_inc(s_ident, 1)
            nc.gpsimd.memset(ident[:, :], 0.0).then_inc(s_ident, 1)
            pool.wait_ge(s_ident, 2)
            nc.gpsimd.affine_select(out=ident[:, :], in_=ident[:, :], compare_op=ALU.not_equal, fill=1.0,
                                    base=0, pattern=[[-1, P]], channel_multiplier=1).then_inc(s_ident, 1)
            nc.gpsimd.memset(v_hi[:, :, :, D:V1], 1.0).then_inc(s_ones, 1)

            def residual(m, s, ahead):
                parity, a = pair_of(s, ahead)
                place = (m % RING if isinstance(m, int) else m & (RING - 1)) * H
                nc.gpsimd.tensor_tensor(resid[:, bass.ds(place, H)], x_in[:, parity, a, :], out_bias[:, :],
                                        ALU.add).then_inc(s_resid, 1)

            def slot(g, s):
                if isinstance(g, int) and g == FIRST + EARLY:
                    pool.wait_ge(s_out_bias, 1)
                    pool.wait_ge(s_kept, EARLY)
                    for m in range(EARLY):
                        nc.gpsimd.tensor_tensor(resid[:, m * H:(m + 1) * H], resid[:, m * H:(m + 1) * H],
                                                out_bias[:, :], ALU.add).then_inc(s_resid, 1)
                m = g + NORM_AHEAD
                if has(m):
                    i = at(s, NORM_AHEAD)
                    parity, a = pair_of(s, NORM_AHEAD)
                    col = slice(i, i + 1)
                    done(pool, s_stats, m)
                    done(pool, s_norm, m - 4)
                    nc.gpsimd.tensor_tensor(rstd[:, col], var_eps[:, col], exponent[:, :], ALU.pow).then_inc(s_rstd, 1)
                    done(pool, s_rstd, m)
                    nc.gpsimd.tensor_tensor(shift[:, col], neg_mean[:, col], rstd[:, col], ALU.mult).then_inc(s_shift, 1)
                    done(pool, s_turn_h, m - 4)
                    done(pool, s_shift, m)
                k = g + MASK_AHEAD
                if has(k):
                    mask_parity, mask_a = pair_of(s, MASK_AHEAD)
                    landed(pool, s_adj[mask_parity], k // 4 if isinstance(k, int) else k >> 2)
                    done(pool, s_masked, k - 4)
                if has(m) and (not isinstance(g, int) or g >= FIRST + EARLY):
                    residual(m, s, NORM_AHEAD)
                if has(m):
                    nc.gpsimd.tensor_scalar(x_norm[:, i, :], x_in[:, parity, a, :], rstd[:, col], shift[:, col],
                                            ALU.mult, ALU.add).then_inc(s_norm, 1)
                if has(k):
                    nc.gpsimd.tensor_scalar(mask[:, at(s, MASK_AHEAD), :].rearrange("p (c k) -> p c k", c=C),
                                            adj_in[:, mask_parity, mask_a, :].unsqueeze(1).broadcast_to([P, C, S]),
                                            -NEG, NEG, ALU.mult, ALU.add).then_inc(s_mask, 1)

            first_slots(slot, FIRST, FIRST + 2)
            pool.wait_ge(s_peak, 4)
            nc.gpsimd.partition_all_reduce(peak_qk_all[:, :, :], peak_qk[:, :, :], P, RMAX).then_inc(s_peak_all, 1)
            first_slots(slot, FIRST + 2, FIRST + EARLY)
            pool.wait_ge(s_peak, 6)
            nc.gpsimd.partition_all_reduce(peak_vf_all[:, :], peak_vf[:, :], P, RMAX).then_inc(s_peak_all, 1)
            run_slots(pool, slot, FIRST + EARLY)

        @block.scalar
        def _(act):
            for i, b in enumerate((bq, bk)):
                act.dma_start(b_raw[:, i, :], b.rearrange("(c p) -> p c", p=P),
                              allow_slow_non_contiguous=True).then_inc(s_bqk, 16)
            for i, w in ((1, Wk), (3, Wf)):
                act.dma_start(w_raw[:, i, :, :], w.rearrange("(c p) n -> p c n", p=P)).then_inc(s_weights[i], 16)

            def matrix_hi(i):
                act.wait_ge(s_w_scale, 1 + i // 2)
                nc.scalar.activation(w_hi[:, i, :, :], w_raw[:, i, :, :], ACT.Copy,
                                     scale=w_scale[:, i:i + 1]).then_inc(s_w_hi[i], 1)

            def slot(g, s):
                k = g + PROJ_AHEAD
                parity, a = pair_of(s, PROJ_AHEAD)
                mix = g - MIX_BEHIND

                def chunk(c):
                    if has(k):
                        done(act, s_chunk[c], k)
                        nc.scalar.activation(qk_hi[:, parity, a, c, :], proj_bank(s, c)[:, 0:PAIR], ACT.Identity,
                                             bias=b_up[:, a, c:c + 1]).then_inc(s_chunk_hi[c], 1)

                if has(mix):
                    done(act, s_turn_p, mix)
                    nc.scalar.activation(pt_hi[:, :, :], pt, ACT.Copy).then_inc(s_pt_hi, 1)
                chunk(0)
                chunk(1)
                if isinstance(g, int) and g == FIRST + EARLY:
                    matrix_hi(2)
                    matrix_hi(1)
                if has(g + HT_AHEAD):
                    hp, ha = pair_of(s, HT_AHEAD)
                    done(act, s_turn_h, g + HT_AHEAD)
                    nc.scalar.activation(h_hi[:, hp, :, ha * S:(ha + 1) * S], turn, ACT.Relu).then_inc(s_h_hi, 1)
                chunk(2)
                if has(g):
                    done(act, s_max, g)
                    for r in range(2):
                        for c in range(C):
                            last = nc.scalar.activation(probs[:, r, c, :], masked[:, r, c * S:(c + 1) * S], ACT.Exp,
                                                        bias=neg_max[:, r, c:c + 1])
                    last.then_inc(s_exp, 1)
                if has(k):
                    done(act, s_v, k)
                    if isinstance(k, int) and k == 0:
                        act.wait_ge(s_ones, 1)
                    nc.scalar.activation(v_hi[:, at(s, PROJ_AHEAD), :, 0:D],
                                         proj_bank(s, 3)[:, 0:H].rearrange("p (h d) -> p h d", h=HEADS),
                                         ACT.Copy).then_inc(s_v_hi, 1)
                if has(mix):
                    done(act, s_turn_c, mix)
                    nc.scalar.activation(ct_hi[:, :, :], turn, ACT.Copy).then_inc(s_ct_hi, 1)

            for m in range(EARLY):
                act.wait_ge(s_x[m // 2], 16)
                nc.scalar.activation(resid[:, m * H:(m + 1) * H], x_in[:, m // 2, m % 2, :], ACT.Copy).then_inc(s_kept, 1)
            act.wait_ge(s_bv, 16)
            nc.scalar.copy(bv_wide[:, :, :], b_raw[:, 2, :].unsqueeze(2).broadcast_to([P, C, P])).then_inc(s_bv_wide, 1)
            first_slots(slot, FIRST, FIRST + EARLY)
            matrix_hi(0)
            act.wait_ge(s_b_up, 2)
            first_slots(slot, FIRST + EARLY, FIRST + EARLY + 1)
            matrix_hi(3)
            run_slots(act, slot, FIRST + EARLY + 1)

        @block.vector
        def _(dve):
            def rest(i):
                dve.wait_ge(s_w_hi[i], 1)
                nc.vector.scalar_tensor_tensor(w_lo[:, i, :, :].rearrange("p c n -> p (c n)"),
                                               w_raw[:, i, :, :].rearrange("p c n -> p (c n)"), w_scale[:, i:i + 1],
                                               w_hi[:, i, :, :].rearrange("p c n -> p (c n)"), ALU.mult,
                                               ALU.subtract).then_inc(s_w_lo[i], 1)

            def slot(g, s):
                k = g + PROJ_AHEAD
                parity, a = pair_of(s, PROJ_AHEAD)
                mix = g - MIX_BEHIND

                def chunk(c):
                    if has(k):
                        done(dve, s_chunk_hi[c], k)
                        nc.vector.scalar_tensor_tensor(qk_lo[:, parity, a, c, :], proj_bank(s, c)[:, 0:PAIR],
                                                       b_up[:, a, c:c + 1], qk_hi[:, parity, a, c, :], ALU.add,
                                                       ALU.subtract).then_inc(s_chunk_lo[c], 1)

                def mask_scores(g, s):
                    done(dve, s_scores, g)
                    done(dve, s_mask, g)
                    done(dve, s_exp, g - 1)
                    nc.vector.scalar_tensor_tensor(masked[:, :, :], ps_scores[:, :, 0:C * S], score_scale,
                                                   mask[:, at(s, 0), :].unsqueeze(1).broadcast_to([P, 2, C * S]),
                                                   ALU.mult, ALU.add).then_inc(s_masked, 1)

                def maxima(g):
                    done(dve, s_masked, g)
                    nc.vector.tensor_reduce(neg_max[:, :, :], masked[:, :, :].rearrange("p r (c k) -> p r c k", c=C),
                                            AX_X, ALU.max, negate=True).then_inc(s_max, 1)

                m = g + NORM_AHEAD
                if has(m):
                    i = at(s, NORM_AHEAD)
                    xp, xa = pair_of(s, NORM_AHEAD)
                    landed(dve, s_x[xp], m // 4 if isinstance(m, int) else m >> 2)
                    nc.vector.bn_stats(stats[:, i, :], x_in[:, xp, xa, :]).then_inc(s_moments, 1)
                if has(mix):
                    done(dve, s_pt_hi, mix)
                    nc.vector.tensor_tensor(pt_lo[:, :, :], pt, pt_hi[:, :, :], ALU.subtract).then_inc(s_pt_lo, 1)
                chunk(0)
                if usual(g):
                    mask_scores(g, s)
                chunk(1)
                if usual(g):
                    maxima(g)
                if isinstance(g, int) and g == FIRST + EARLY:
                    rest(2)
                    rest(1)
                    dve.wait_ge(s_bvwf, 1)
                    dve.wait_ge(s_bf, 16)
                    nc.vector.tensor_tensor(out_bias[:, :], ps_ctx[:, 0:H], bf_rows[:, :], ALU.add).then_inc(s_out_bias, 1)
                chunk(2)
                if has(g + HT_AHEAD):
                    hp, ha = pair_of(s, HT_AHEAD)
                    part = slice(ha * S, (ha + 1) * S)
                    done(dve, s_h_hi, g + HT_AHEAD)
                    nc.vector.scalar_tensor_tensor(h_lo[:, hp, :, part], turn, 0.0, h_hi[:, hp, :, part], ALU.max,
                                                   ALU.subtract).then_inc(s_h_lo, 1)
                if has(m):
                    done(dve, s_moments, m)
                if has(mix):
                    done(dve, s_pv, mix)
                    nc.vector.reciprocal(inv_sum[:, :], ctx_sum[:, :, D]).then_inc(s_inv, 1)
                    done(dve, s_inv, mix)
                    nc.vector.tensor_tensor(context[:, :].rearrange("p (h d) -> p h d", h=HEADS), ctx_sum[:, :, 0:D],
                                            inv_sum[:, :].unsqueeze(2).broadcast_to([P, HEADS, D]),
                                            ALU.mult).then_inc(s_context, 1)
                if pulled(g + 1):
                    mask_scores(g + 1, s + 1)
                    maxima(g + 1)
                if has(m):
                    nc.vector.bn_aggr(mean_var[:, i, :], stats[:, i, :]).then_inc(s_mean_var, 1)
                if has(k):
                    done(dve, s_v_hi, k)
                    vi = at(s, PROJ_AHEAD)
                    nc.vector.tensor_tensor(v_lo[:, vi, :, 0:D],
                                            proj_bank(s, 3)[:, 0:H].rearrange("p (h d) -> p h d", h=HEADS),
                                            v_hi[:, vi, :, 0:D], ALU.subtract).then_inc(s_v_lo, 1)
                if has(m):
                    done(dve, s_shift, m - 4)
                    done(dve, s_mean_var, m)
                    nc.vector.tensor_scalar(var_eps[:, i:i + 1], mean_var[:, i, 1:2], H_UP ** -2, EPS * H_UP ** -2,
                                            ALU.mult, ALU.add)
                    nc.vector.tensor_scalar(neg_mean[:, i:i + 1], mean_var[:, i, 0:1], -1.0, None,
                                            ALU.mult).then_inc(s_stats, 1)
                y = g - OUT_BEHIND
                if has(y):
                    op, oa = pair_of(s, -OUT_BEHIND)
                    done(dve, s_y, y)
                    done(dve, s_resid, y)
                    landed(dve, s_store[op], y // 4 - 1 if isinstance(y, int) else (y >> 2) - 1)
                    place = (y % RING if isinstance(y, int) else y & (RING - 1)) * H
                    nc.vector.scalar_tensor_tensor(y_out[:, op, oa, :], proj_bank(s, 4)[:, 0:H], out_scale,
                                                   resid[:, bass.ds(place, H)], ALU.mult, ALU.add).then_inc(s_out, 1)
                if has(mix):
                    done(dve, s_ct_hi, mix)
                    nc.vector.tensor_tensor(ct_lo[:, :, :], turn, ct_hi[:, :, :], ALU.subtract).then_inc(s_ct_lo, 1)

            first_slots(slot, FIRST, FIRST + 2)

            def matrix_peak(i, to):
                dve.wait_ge(s_weights[i], 16)
                nc.vector.tensor_reduce(to, w_raw[:, i, :, :].rearrange("p c n -> p (c n)"), AX_X, ALU.max,
                                        apply_absolute_value=True).then_inc(s_peak, 1)

            def scales(first, peaks, step):
                two = slice(first, first + 2)
                nc.vector.tensor_scalar(size[:, two], peaks, 2.0 ** -30, 2.0 ** 40, ALU.max, ALU.min).then_inc(s_scale, 1)
                dve.wait_ge(s_scale, step + 1)
                nc.vector.tensor_scalar(pow2[:, two].bitcast(U32), size[:, two].bitcast(U32), 0x7F800000, None,
                                        ALU.bitwise_and).then_inc(s_scale, 1)
                dve.wait_ge(s_scale, step + 2)
                nc.vector.reciprocal(pow2_inv[:, two], pow2[:, two]).then_inc(s_scale, 1)
                dve.wait_ge(s_scale, step + 3)
                nc.vector.tensor_scalar(w_scale[:, two], pow2_inv[:, two], W_UP, None, ALU.mult).then_inc(s_w_scale, 1)

            for i in range(2):
                matrix_peak(i, peak_qk[:, 0, i:i + 1])
                if i == 0:
                    first_slots(slot, FIRST + 2, FIRST + 3)
            dve.wait_ge(s_bqk, 32)
            nc.vector.tensor_reduce(peak_qk[:, 1, :], b_raw[:, 0:2, :], AX_X, ALU.max,
                                    apply_absolute_value=True).then_inc(s_peak, 1)
            dve.wait_ge(s_peak, 3)
            nc.vector.tensor_scalar(peak_qk[:, 1, :], peak_qk[:, 1, :], 1.0 / P, None, ALU.mult).then_inc(s_peak, 1)
            first_slots(slot, FIRST + 3, FIRST + EARLY)
            dve.wait_ge(s_peak_all, 1)
            nc.vector.tensor_tensor(peak_qk_all[:, 0, :], peak_qk_all[:, 0, :], peak_qk_all[:, 1, :],
                                    ALU.max).then_inc(s_scale, 1)
            dve.wait_ge(s_scale, 1)
            scales(0, peak_qk_all[:, 0, :], 1)
            for i in range(2):
                nc.vector.tensor_scalar(b_up[:, i, :], b_raw[:, i, :], pow2_inv[:, i:i + 1], UP, ALU.mult,
                                        ALU.mult).then_inc(s_b_up, 1)
            nc.vector.scalar_tensor_tensor(score_scale, pow2[:, 0:1], 1.0 / (UP * UP * D ** 0.5), pow2[:, 1:2],
                                           ALU.mult, ALU.mult).then_inc(s_consts, 1)
            matrix_peak(2, peak_vf[:, 0:1])
            rest(0)
            matrix_peak(3, peak_vf[:, 1:2])
            dve.wait_ge(s_peak_all, 2)
            scales(2, peak_vf_all[:, :], 4)
            nc.vector.scalar_tensor_tensor(out_scale, pow2[:, 2:3], 1.0 / (UP * W_UP), pow2[:, 3:4],
                                           ALU.mult, ALU.mult).then_inc(s_consts, 1)
            dve.wait_ge(s_b_up, 2)
            dve.wait_ge(s_consts, 2)
            first_slots(slot, FIRST + EARLY, FIRST + EARLY + 1)
            rest(3)
            run_slots(dve, slot, FIRST + EARLY + 1)

        @block.tensor
        def _(pe):
            pe.wait_ge(s_ident, 3)

            def slot(g, s):
                k = g + PROJ_AHEAD
                parity, a = pair_of(s, PROJ_AHEAD)
                mix = g - MIX_BEHIND
                y = g - OUT_BEHIND

                def weights_ready(matrix):
                    if isinstance(g, int) and g <= OUT_BEHIND:
                        pe.wait_ge(s_w_lo[matrix], 1)

                def chunk(c):
                    feats = slice(c * P, (c + 1) * P)
                    pairs = []
                    for i in range(C):
                        pairs += [(w_hi[:, a, i, feats], h_hi[:, parity, i, :]),
                                  (w_hi[:, a, i, feats], h_lo[:, parity, i, :]),
                                  (w_lo[:, a, i, feats], h_hi[:, parity, i, :])]
                    weights_ready(a)
                    split_matmuls(proj_bank(s, c)[:, 0:PAIR], pairs, True, True).then_inc(s_chunk[c], 1)

                def output(y, s):
                    done(pe, s_ct_lo, y)
                    if has(k):
                        done(pe, s_chunk_lo[2], k)
                    else:
                        done(pe, s_out, y - 1)
                    pairs = []
                    for c in range(C):
                        pairs += [(ct_hi[:, c, :], w_hi[:, 3, c, :]),
                                  (ct_lo[:, c, :], w_hi[:, 3, c, :]),
                                  (ct_hi[:, c, :], w_lo[:, 3, c, :])]
                    weights_ready(3)
                    split_matmuls(proj_bank(s, 4)[:, 0:H], pairs, True, True).then_inc(s_y, 1)

                def score(g, s):
                    cur, half = pair_of(s, 0)
                    if half == 0:
                        done(pe, s_chunk_lo[2], g + 1)
                    done(pe, s_masked, g - 1)
                    tok = slice(half * S, (half + 1) * S)
                    for c in range(C):
                        for i, (q, kk) in enumerate(((qk_hi, qk_hi), (qk_lo, qk_hi), (qk_hi, qk_lo))):
                            for r in range(2):
                                rows = slice(r * D, (r + 1) * D)
                                last = nc.tensor.matmul(scores[:, r, c, :], q[rows, cur, 0, c, tok],
                                                        kk[rows, cur, 1, c, tok], start=(i == 0), stop=(i == 2))
                    last.then_inc(s_scores, 1)

                if has(mix):
                    done(pe, s_exp, mix)
                    done(pe, s_pt_lo, mix - 1)
                    for h in range(HEADS):
                        last = nc.tensor.transpose(pt[:, h, :], probs[:, h % 2, h // 2, :], ident[:, :])
                    last.then_inc(s_turn_p, 1)
                if has(k):
                    if a == 0:
                        done(pe, s_h_lo, k + 1)
                    done(pe, s_v_lo, k - 1)
                    chunk(0)
                if usual(g):
                    score(g, s)
                if has(k):
                    done(pe, s_out, y - 1)
                    chunk(1)
                if has(g + HT_AHEAD):
                    done(pe, s_norm, g + HT_AHEAD)
                    done(pe, s_ct_lo, mix - 1)
                    if isinstance(g, int) and not has(mix - 1):
                        done(pe, s_h_lo, g + HT_AHEAD - 1)
                    for c in range(C):
                        last = nc.tensor.transpose(turn[:, c, :], x_norm[:, at(s, HT_AHEAD), c * P:(c + 1) * P],
                                                   ident[:, :])
                    last.then_inc(s_turn_h, 1)
                if has(k):
                    done(pe, s_chunk_lo[0], k)
                    chunk(2)
                if has(y) and not has(k):
                    output(y, s)
                if has(mix):
                    done(pe, s_pt_lo, mix)
                    done(pe, s_v_lo, mix)
                    done(pe, s_context, mix - 1)
                    vi = at(s, -MIX_BEHIND)
                    for h in range(HEADS):
                        nc.tensor.matmul(ctx_sum[:, h, :], pt_hi[:, h, :], v_hi[:, vi, h, :], start=True, stop=False)
                        nc.tensor.matmul(ctx_sum[:, h, :], pt_lo[:, h, :], v_hi[:, vi, h, :], start=False, stop=False)
                        last = nc.tensor.matmul(ctx_sum[:, h, 0:D], pt_hi[:, h, :], v_lo[:, vi, h, 0:D], start=False,
                                                stop=True)
                    last.then_inc(s_pv, 1)
                if pulled(g + 1):
                    score(g + 1, s + 1)
                if has(k):
                    done(pe, s_chunk_lo[1], k)
                    tok = slice(a * S, (a + 1) * S)
                    pairs = []
                    for i in range(C):
                        pairs += [(h_hi[:, parity, i, tok], w_hi[:, 2, i, :]),
                                  (h_lo[:, parity, i, tok], w_hi[:, 2, i, :]),
                                  (h_hi[:, parity, i, tok], w_lo[:, 2, i, :])]
                    weights_ready(2)
                    split_matmuls(proj_bank(s, 3)[:, 0:H], pairs, True, True).then_inc(s_v, 1)
                if has(y) and has(k):
                    output(y, s)
                if has(mix):
                    done(pe, s_context, mix)
                    if has(g + HT_AHEAD):
                        done(pe, s_h_lo, g + HT_AHEAD)
                    else:
                        done(pe, s_ct_lo, mix - 1)
                    for c in range(C):
                        last = nc.tensor.transpose(turn[:, c, :], context[:, c * P:(c + 1) * P], ident[:, :])
                    last.then_inc(s_turn_c, 1)

            first_slots(slot, FIRST, FIRST + EARLY)
            pe.wait_ge(s_weights[3], 16)
            pe.wait_ge(s_bv_wide, 1)
            for c in range(C):
                last = nc.tensor.matmul(ps_ctx[:, 0:H], bv_wide[:, c, :], w_raw[:, 3, c, :], start=(c == 0),
                                        stop=(c == C - 1))
            last.then_inc(s_bvwf, 1)
            run_slots(pe, slot, FIRST + EARLY)


_INS = ['x', 'adj', 'L0_gnn_Wq', 'L0_gnn_bq', 'L0_gnn_Wk', 'L0_gnn_bk', 'L0_gnn_Wv', 'L0_gnn_bv', 'L0_gnn_Wf',
        'L0_gnn_bf']
_OUTS = [((128, 128, 384), 'float32')]


def kernel(**inputs):
    import numpy as _np
    import concourse.bacc as _bacc
    from concourse import mybir as _mybir
    from concourse.bass_utils import run_bass_kernel_spmd as _run

    nc = _bacc.Bacc("TRN2", target_bir_lowering=False, num_devices=1)
    arrays, args = {}, []
    for name in _INS:
        a = _np.ascontiguousarray(inputs[name])
        arrays[f"in_{name}_dram"] = a
        args.append(nc.dram_tensor(f"in_{name}_dram", a.shape, _mybir.dt.from_np(a.dtype), kind="ExternalInput").ap())
    for i, (shape, dtype) in enumerate(_OUTS):
        dt = _mybir.dt.from_np(_np.dtype(dtype))
        args.append(nc.dram_tensor(f"out_{i}_dram", shape, dt, kind="ExternalOutput").ap())
    gnn_kernel(nc, *args)
    r = _run(nc, [arrays], core_ids=[0])
    got = tuple(r.results[0][f"out_{i}_dram"] for i in range(len(_OUTS)))
    return got[0]
```
